# Optimizing a Trainium2 kernel written in Bass

```python
import numpy as np
import jax
import jax.numpy as jnp

def _softmax(x, axis=-1):
    return jax.nn.softmax(x, axis=axis)

def _gelu(x):
    return jax.nn.gelu(x, approximate=True)

def _silu(x):
    return jax.nn.silu(x)

def _sigmoid(x):
    return jax.nn.sigmoid(x)

def _layernorm(x, axis=-1, eps=1e-05):
    m = jnp.mean(x, axis=axis, keepdims=True)
    v = jnp.var(x, axis=axis, keepdims=True)
    return (x - m) / jnp.sqrt(v + eps)

def _scatter_add(tgt, idx, src, axis=0):
    return tgt.at[idx].add(src)

def _segment_sum(src, seg, n):
    return jax.ops.segment_sum(src, seg, n)
kernel_name = 'mk_cond_resid_d2_seqx_r4_93dc9a'

def setup_inputs(seed: int=0):
    np.random.seed(seed)
    _w = jnp.asarray

    def _rec_inputs():
        import jax
        import jax.numpy as jnp
        _rk = jax.random.key(seed)
        x = 7.22e-05 + 1 * jax.random.normal(jax.random.fold_in(_rk, 1), (16, 256, 256), jnp.float32)
        _lenS = 256 - jax.random.randint(jax.random.fold_in(_rk, 7), (16,), 0, max(1, 256 // 4) + 1, jnp.int32)
        _lenS2 = 256 - jax.random.randint(jax.random.fold_in(_rk, 8), (16,), 0, max(1, 256 // 4) + 1, jnp.int32)
        cond_256 = 0.000887014 + 1.03683 * jax.random.normal(jax.random.fold_in(_rk, 11), (16, 64), jnp.float32)
        _validS = jnp.arange(256)[None, :] < _lenS[:, None]
        _validS2 = jnp.arange(256)[None, :] < _lenS2[:, None]
        _causal = jnp.tril(jnp.ones((256, 256), dtype=bool))
        mask_SxS_bk1 = jnp.broadcast_to(_validS[0:1, :], (256, 256))
        return (x, cond_256, mask_SxS_bk1)
    x, cond_256, mask_SxS_bk1 = _rec_inputs()

    def _L0_cond_setup():
        import jax, jax.numpy as jnp
        import numpy as np
        D_MODEL = 256
        D_T = 64
        N_HEADS = 16
        HIDDEN = 4 * D_MODEL
        EPS = 1e-06

        def _tc_rmsnorm(x, t, gw, gb, bw, bb):
            g = (t @ gw.T + gb)[:, None, :]
            b = (t @ bw.T + bb)[:, None, :]
            inv_rms = jax.lax.rsqrt(jnp.mean(x * x, axis=-1, keepdims=True) + EPS)
            return g * x * inv_rms + b

        def _attention(x, Wq, Wk, Wv, Wo):
            B, L, D = x.shape
            H = N_HEADS
            dh = D // H
            scale = np.sqrt(dh).astype(np.float32)
            q = (x @ Wq.T).reshape(B, L, H, dh)
            k = (x @ Wk.T).reshape(B, L, H, dh)
            v = (x @ Wv.T).reshape(B, L, H, dh)
            attn = jnp.einsum('blhd,bmhd->bhlm', q, k) / scale
            p = jax.nn.softmax(attn, axis=-1)
            o = jnp.einsum('bhlm,bmhd->blhd', p, v).reshape(B, L, D)
            return o @ Wo.T

        def _swiglu(x, gate_w, hid_w, out_w):
            return jax.nn.silu(x @ gate_w.T) * (x @ hid_w.T) @ out_w.T
        key = jax.random.key(seed)
        ks = jax.random.split(key, 20)
        B, L = (8, 256)
        s_d = 1.0 / np.sqrt(D_MODEL)
        s_t = 1.0 / np.sqrt(D_T)
        s_h = 1.0 / np.sqrt(HIDDEN)
        return {'x': jax.random.normal(ks[0], (B, L, D_MODEL), jnp.float32), 't': jax.random.normal(ks[1], (B, D_T), jnp.float32), 'Wq': jax.random.normal(ks[2], (D_MODEL, D_MODEL), jnp.float32) * s_d, 'Wk': jax.random.normal(ks[3], (D_MODEL, D_MODEL), jnp.float32) * s_d, 'Wv': jax.random.normal(ks[4], (D_MODEL, D_MODEL), jnp.float32) * s_d, 'Wo': jax.random.normal(ks[5], (D_MODEL, D_MODEL), jnp.float32) * s_d, 'g1w': jax.random.normal(ks[6], (D_MODEL, D_T), jnp.float32) * s_t, 'g1b': jnp.ones((D_MODEL,), jnp.float32), 'b1w': jax.random.normal(ks[7], (D_MODEL, D_T), jnp.float32) * s_t, 'b1b': jnp.zeros((D_MODEL,), jnp.float32), 'g2w': jax.random.normal(ks[8], (D_MODEL, D_T), jnp.float32) * s_t, 'g2b': jnp.ones((D_MODEL,), jnp.float32), 'b2w': jax.random.normal(ks[9], (D_MODEL, D_T), jnp.float32) * s_t, 'b2b': jnp.zeros((D_MODEL,), jnp.float32), 'gate_w': jax.random.normal(ks[10], (HIDDEN, D_MODEL), jnp.float32) * s_d, 'hid_w': jax.random.normal(ks[11], (HIDDEN, D_MODEL), jnp.float32) * s_d, 'out_w': jax.random.normal(ks[12], (D_MODEL, HIDDEN), jnp.float32) * s_h}
    _L0_cond_all = _L0_cond_setup()
    _L0_cond_in = {k: v for k, v in _L0_cond_all.items() if k in ('Wq', 'Wk', 'Wv', 'Wo', 'g1w', 'g1b', 'b1w', 'b1b', 'g2w', 'g2b', 'b2w', 'b2b', 'gate_w', 'hid_w', 'out_w')}
    del _L0_cond_all

    def _L1_cond_setup():
        import jax, jax.numpy as jnp
        import numpy as np
        EPS = 1e-06
        key = jax.random.key(seed)
        ks = jax.random.split(key, 8)
        B, S, E, C = (2, 512, 256, 64)
        x = jax.random.normal(ks[0], (B, S, E), dtype=jnp.float32)
        mask = jnp.triu(jnp.ones((S, S), dtype=bool), k=1)
        conditioning = jax.random.normal(ks[1], (B, C), dtype=jnp.float32)
        sc = 1.0 / np.sqrt(E)
        Wq = jax.random.normal(ks[2], (E, E), dtype=jnp.float32) * sc
        Wk = jax.random.normal(ks[3], (E, E), dtype=jnp.float32) * sc
        Wv = jax.random.normal(ks[4], (E, E), dtype=jnp.float32) * sc
        Wo = jax.random.normal(ks[5], (E, E), dtype=jnp.float32) * sc
        rms_scale = jnp.ones((E,), dtype=jnp.float32)
        Wc = jax.random.normal(ks[6], (2 * E, C), dtype=jnp.float32) * 0.02
        bc = jax.random.normal(ks[7], (2 * E,), dtype=jnp.float32) * 0.02
        return {'x': x, 'mask': mask, 'conditioning': conditioning, 'Wq': Wq, 'Wk': Wk, 'Wv': Wv, 'Wo': Wo, 'rms_scale': rms_scale, 'Wc': Wc, 'bc': bc}
    _L1_cond_all = _L1_cond_setup()
    _L1_cond_in = {k: v for k, v in _L1_cond_all.items() if k in ('Wq', 'Wk', 'Wv', 'Wo', 'rms_scale', 'Wc', 'bc')}
    del _L1_cond_all
    return {'x': x, 'cond_256': cond_256, 'mask_SxS_bk1': mask_SxS_bk1, 'L0_cond_Wq': _L0_cond_in['Wq'], 'L0_cond_Wk': _L0_cond_in['Wk'], 'L0_cond_Wv': _L0_cond_in['Wv'], 'L0_cond_Wo': _L0_cond_in['Wo'], 'L0_cond_g1w': _L0_cond_in['g1w'], 'L0_cond_g1b': _L0_cond_in['g1b'], 'L0_cond_b1w': _L0_cond_in['b1w'], 'L0_cond_b1b': _L0_cond_in['b1b'], 'L0_cond_g2w': _L0_cond_in['g2w'], 'L0_cond_g2b': _L0_cond_in['g2b'], 'L0_cond_b2w': _L0_cond_in['b2w'], 'L0_cond_b2b': _L0_cond_in['b2b'], 'L0_cond_gate_w': _L0_cond_in['gate_w'], 'L0_cond_hid_w': _L0_cond_in['hid_w'], 'L0_cond_out_w': _L0_cond_in['out_w'], 'L1_cond_Wq': _L1_cond_in['Wq'], 'L1_cond_Wk': _L1_cond_in['Wk'], 'L1_cond_Wv': _L1_cond_in['Wv'], 'L1_cond_Wo': _L1_cond_in['Wo'], 'L1_cond_rms_scale': _L1_cond_in['rms_scale'], 'L1_cond_Wc': _L1_cond_in['Wc'], 'L1_cond_bc': _L1_cond_in['bc']}

def reference(x, cond_256, mask_SxS_bk1, L0_cond_Wq, L0_cond_Wk, L0_cond_Wv, L0_cond_Wo, L0_cond_g1w, L0_cond_g1b, L0_cond_b1w, L0_cond_b1b, L0_cond_g2w, L0_cond_g2b, L0_cond_b2w, L0_cond_b2b, L0_cond_gate_w, L0_cond_hid_w, L0_cond_out_w, L1_cond_Wq, L1_cond_Wk, L1_cond_Wv, L1_cond_Wo, L1_cond_rms_scale, L1_cond_Wc, L1_cond_bc):
    import jax
    import jax.numpy as jnp

    def _L0_cond_ref(x, t, Wq, Wk, Wv, Wo, g1w, g1b, b1w, b1b, g2w, g2b, b2w, b2b, gate_w, hid_w, out_w):
        import jax, jax.numpy as jnp
        import numpy as np
        D_MODEL = 256
        D_T = 64
        N_HEADS = 16
        HIDDEN = 4 * D_MODEL
        EPS = 1e-06

        def _tc_rmsnorm(x, t, gw, gb, bw, bb):
            g = (t @ gw.T + gb)[:, None, :]
            b = (t @ bw.T + bb)[:, None, :]
            inv_rms = jax.lax.rsqrt(jnp.mean(x * x, axis=-1, keepdims=True) + EPS)
            return g * x * inv_rms + b

        def _attention(x, Wq, Wk, Wv, Wo):
            B, L, D = x.shape
            H = N_HEADS
            dh = D // H
            scale = np.sqrt(dh).astype(np.float32)
            q = (x @ Wq.T).reshape(B, L, H, dh)
            k = (x @ Wk.T).reshape(B, L, H, dh)
            v = (x @ Wv.T).reshape(B, L, H, dh)
            attn = jnp.einsum('blhd,bmhd->bhlm', q, k) / scale
            p = jax.nn.softmax(attn, axis=-1)
            o = jnp.einsum('bhlm,bmhd->blhd', p, v).reshape(B, L, D)
            return o @ Wo.T

        def _swiglu(x, gate_w, hid_w, out_w):
            return jax.nn.silu(x @ gate_w.T) * (x @ hid_w.T) @ out_w.T
        x = x + _attention(_tc_rmsnorm(x, t, g1w, g1b, b1w, b1b), Wq, Wk, Wv, Wo)
        return x + _swiglu(_tc_rmsnorm(x, t, g2w, g2b, b2w, b2b), gate_w, hid_w, out_w)

    def _L1_cond_ref(x, mask, conditioning, Wq, Wk, Wv, Wo, rms_scale, Wc, bc):
        import jax, jax.numpy as jnp
        import numpy as np
        EPS = 1e-06
        B, S, E = x.shape
        H = 16
        D = E // H
        scale = D ** (-0.5)

        def proj(W):
            return (x @ W.T).reshape(B, S, H, D).transpose(0, 2, 1, 3)
        q, k, v = (proj(Wq), proj(Wk), proj(Wv))
        scores = jnp.einsum('bhsd,bhtd->bhst', q, k) * scale
        scores = jnp.where(mask[None, None, :, :], -jnp.inf, scores)
        attn = jax.nn.softmax(scores, axis=-1)
        out = jnp.einsum('bhst,bhtd->bhsd', attn, v)
        out = out.transpose(0, 2, 1, 3).reshape(B, S, E)
        out = out @ Wo.T
        rms = jnp.sqrt(jnp.mean(out * out, axis=-1, keepdims=True) + EPS)
        xn = out / rms * rms_scale
        mod = jax.nn.silu(conditioning) @ Wc.T + bc
        shift, sc = jnp.split(mod, 2, axis=-1)
        xn = xn * (1.0 + sc[:, None, :]) + shift[:, None, :]
        return xn
    x = x + _L0_cond_ref(x, cond_256, L0_cond_Wq, L0_cond_Wk, L0_cond_Wv, L0_cond_Wo, L0_cond_g1w, L0_cond_g1b, L0_cond_b1w, L0_cond_b1b, L0_cond_g2w, L0_cond_g2b, L0_cond_b2w, L0_cond_b2b, L0_cond_gate_w, L0_cond_hid_w, L0_cond_out_w)
    x = x + _L1_cond_ref(x, mask_SxS_bk1, cond_256, L1_cond_Wq, L1_cond_Wk, L1_cond_Wv, L1_cond_Wo, L1_cond_rms_scale, L1_cond_Wc, L1_cond_bc)
    return x

_drawn_inputs = setup_inputs


def setup_inputs(seed=0):
    import zlib

    import numpy as np

    out = dict(_drawn_inputs(seed))
    spreads = {'L0_cond_g1b': (1.0, 0.2),
     'L0_cond_b1b': (0.0, 0.1),
     'L0_cond_g2b': (1.0, 0.2),
     'L0_cond_b2b': (0.0, 0.1),
     'L1_cond_rms_scale': (1.0, 0.2)}
    factors = {'L1_cond_bc': 6.626}
    for name, (base, spread) in spreads.items():
        noise = np.random.default_rng([zlib.crc32(name.encode()), seed]).standard_normal(out[name].shape)
        drawn = base * np.exp(spread * noise) if base else spread * noise
        out[name] = jnp.asarray(drawn.astype(out[name].dtype))
    for name, factor in factors.items():
        out[name] = (out[name] * factor).astype(out[name].dtype)
    return out
```

```python
from contextlib import ExitStack

import concourse.bass as bass
from concourse import mybir

F32 = mybir.dt.float32
F32R = mybir.dt.float32r
BF16 = mybir.dt.bfloat16
I32 = mybir.dt.int32
U8 = mybir.dt.uint8
ACT = mybir.ActivationFunctionType
ALU = mybir.AluOpType
AX_X = mybir.AxisListType.X

P = 128
B = 16
T = 256
D = 256
H = 16
DH = D // H
HID = 1024
FC = D // P
TC = T // P
HC = HID // P
DT = 64
EPS = 1e-6
SCORE_SCALE = DH ** -0.5
PARTS = 6 * DH
ROWS = PARTS + 3
SLOTS = 8
UNITS = 16
E_RING = 8
VW = 32
NEG = -1.0e38
CLAMP = 5.0e37
RSQRT_MAGIC = float(0x5F3759DF)
NEWTON_OPS = 11
SHIFT_OPS = 4
FIRST, LAST = -3, 2 * B

C_G1, C_B1, C_G2, C_B2, C_SHIFT, C_SCALE = 0, 2, 4, 6, 8, 10
CCH = 12


def stages(s):
    def layer(n):
        return None if n < 0 or n >= 2 * B else n // B
    at = {"N": s + 3, "A": s + 2, "V": s + 1, "B1": s + 1, "B2": s, "C": s - 1}
    found = {k: layer(n) for k, n in at.items()}
    found["C2"] = 0 if layer(s - 2) == 0 else None
    return found


def bank_uses(L):
    uses = []
    for g in range(SLOTS):
        if L["C2"] is not None:
            uses.append(f"F{g}")
        if g == 0 and L["C"] is not None:
            uses += ["T1a", "T1b"]
        if g == 1:
            uses += ["T2"] * (L["C"] is not None) + ["V"] * (L["V"] is not None)
        if g == 2:
            uses += ["Wo"] * (L["C"] is not None) + ["Q"] * (L["A"] is not None)
        if g == 3 and L["A"] is not None:
            uses.append("K")
        if g == 4:
            uses += ["ms"] * (L["N"] == 0 or L["C"] is not None) + ["sh0"] * (L["B1"] is not None)
        if g == 6:
            uses += ["bcN"] * (L["N"] == 0) + ["bcC"] * (L["C"] is not None)
    return uses + ["sh1"] * (L["B1"] is not None)


USES_BEFORE = {FIRST: 0}
for _s in range(FIRST, LAST + 1):
    USES_BEFORE[_s + 1] = USES_BEFORE[_s] + len(bank_uses(stages(_s)))


class Step:

    def __init__(self, s0, turn=None):
        self.s0, self.turn = s0, turn
        self.par = s0 % 2
        self.L = stages(s0)
        self.s = s0 if turn is None else turn * 2 + s0

    def n(self, ahead):
        return self.s + ahead

    def last(self):
        return Step(self.s0 - 1, self.turn)

    def bank(self, use):
        k = USES_BEFORE[self.s0] + bank_uses(self.L).index(use)
        before = k // 2
        if self.turn is not None:
            per = (USES_BEFORE[self.s0 + 2] - USES_BEFORE[self.s0]) // 2
            before = self.turn * per + before
        return k % 2, before


def after(eng, sem, count):
    if isinstance(count, int) and count <= 0:
        return
    eng.wait_ge(sem, count)


def run_steps(eng, step):
    for s in range(FIRST, 3):
        step(Step(s))
    with eng.Fori(0, 5) as turn:
        step(Step(3, turn))
        step(Step(4, turn))
    for s in range(13, 19):
        step(Step(s))
    with eng.Fori(0, 5) as turn:
        step(Step(19, turn))
        step(Step(20, turn))
    for s in range(29, LAST + 1):
        step(Step(s))


def build(nc, xT, w0, w_ffn, w_out, w1, condT, cond_w, cond_b, rms_scale, mask, maskT, yT):
    ctx = ExitStack()
    with ctx:
        def sb(name, shape, dt):
            return ctx.enter_context(nc.sbuf_tensor(name, shape, dt))

        def pb(name):
            return ctx.enter_context(nc.psum_tensor(name, [P, 512], F32))

        def sem(name):
            return ctx.enter_context(nc.semaphore(name))

        X = sb("X", [P, B, FC, T], F32)
        Wh = sb("Wh", [P, 4, FC, D], F32R)
        Wl = sb("Wl", [P, 4, FC, D], F32R)
        Gh = sb("Gh", [P, 2, FC, HID], F32R)
        Gl = sb("Gl", [P, 2, FC, HID], F32R)
        Uh = sb("Uh", [P, HC, D], F32R)
        Ul = sb("Ul", [P, HC, D], F32R)
        qst = [sb(f"qst{i}", [P, H, T], BF16) for i in range(2)]
        kst = [sb(f"kst{i}", [P, H, T], BF16) for i in range(2)]
        vaug = [sb(f"vaug{i}", [P, TC, H, VW], F32) for i in range(2)]
        E = sb("E", [P, E_RING, 2 * T], F32)
        nrm = sb("nrm", [P, FC, T], F32)
        xnh = [sb(f"xnh{i}", [P, FC, T], F32R) for i in range(2)]
        xnl = [sb(f"xnl{i}", [P, FC, T], F32R) for i in range(2)]
        dg = sb("dg", [P, 4, P], F32)
        crm = sb("crm", [P, FC, T], F32)
        xch = [sb(f"xch{i}", [P, FC, T], F32R) for i in range(2)]
        xcl = [sb(f"xcl{i}", [P, FC, T], F32R) for i in range(2)]
        rest = sb("rest", [P, FC, T], F32)
        qp = sb("qp", [P, 3, FC, T], BF16)
        kp = sb("kp", [P, 3, FC, T], BF16)
        oT = sb("oT", [P, 4, T], F32)
        on = sb("on", [P, TC, H, DH], F32)
        oh = sb("oh", [P, FC, T], F32R)
        ol = sb("ol", [P, FC, T], F32R)
        y = sb("y", [P, FC, T], F32)
        th = sb("th", [P, 2, T], F32)
        hf = sb("hf", [P, 2, T], F32)
        hh = sb("hh", [P, 2, T], F32R)
        hl = sb("hl", [P, 2, T], F32R)
        msk = sb("msk", [P, TC, T], BF16)
        mskT = sb("mskT", [P, TC, T], BF16)
        ident = sb("ident", [P, P], F32)
        identb = sb("identb", [P, P], BF16)
        ones = sb("ones", [P, P], F32)
        mean1 = sb("mean1", [P, 1], F32)
        cond = sb("cond", [P, CCH, B], F32)
        var = sb("var", [P, 4], F32)
        half = sb("half", [P, 4], F32)
        rstd = sb("rstd", [P, 4], F32)
        tmp4 = sb("tmp4", [P, 4], F32)
        nmax = sb("nmax", [P, 2, TC, 8], F32)
        nrest = sb("nrest", [P, TC, 8], F32)
        nparts = sb("nparts", [P, TC, 3, 8], BF16)
        nT = sb("nT", [24, T], BF16)
        rsum = sb("rsum", [P, TC, H], F32)
        cT = sb("cT", [DT, 2, B], F32)
        cth = sb("cth", [DT, B], F32)
        cb = sb("cb", [P, CCH], F32)
        rs = sb("rs", [P, FC], F32)

        s1ps = [pb(f"s1ps{i}") for i in range(2)]
        s2ps = [pb(f"s2ps{i}") for i in range(2)]
        pvps = pb("pvps")
        work = [pb(f"work{i}") for i in range(2)]
        acc = pb("acc")

        q_scr = [nc.dram_tensor(f"q_scr{i}", (H, 3 * DH, T), BF16, kind="Internal").ap() for i in range(2)]
        k_scr = [nc.dram_tensor(f"k_scr{i}", (H, 3 * DH, T), BF16, kind="Internal").ap() for i in range(2)]
        m_scr = [nc.dram_tensor(f"m_scr{i}", (24, T), BF16, kind="Internal").ap() for i in range(2)]

        x_loaded = sem("x_loaded")
        raw_loaded = [sem(f"raw_loaded{i}") for i in range(2)]
        small_loaded = sem("small_loaded")
        raw_hi = sem("raw_hi")
        raw_lo = sem("raw_lo")
        swap_loaded = sem("swap_loaded")
        swap_hi = sem("swap_hi")
        swap_lo = sem("swap_lo")
        consts = sem("consts")
        stack_ones = sem("stack_ones")
        setup = sem("setup")
        cond_tanh = sem("cond_tanh")
        cond_silu = sem("cond_silu")
        cond_mm = sem("cond_mm")
        cond_ready = sem("cond_ready")
        masks_ready = sem("masks_ready")
        sq_n = sem("sq_n")
        sq_c = sem("sq_c")
        z_ready = sem("z_ready")
        work_full = [sem(f"work_full{i}") for i in range(2)]
        work_free = [sem(f"work_free{i}") for i in range(2)]
        newton = sem("newton")
        diag_ready = sem("diag_ready")
        n_affine = sem("n_affine")
        n_hi = sem("n_hi")
        n_lo = sem("n_lo")
        c_affine = sem("c_affine")
        c_hi = sem("c_hi")
        c_lo = sem("c_lo")
        q_high, q_mid, q_low = sem("q_high"), sem("q_mid"), sem("q_low")
        k_high, k_mid, k_low = sem("k_high"), sem("k_mid"), sem("k_low")
        q_written, k_written = sem("q_written"), sem("k_written")
        stack_loaded = [sem(f"stack_loaded{i}") for i in range(2)]
        s1_full, s1_free = sem("s1_full"), sem("s1_free")
        shift_order, shift_parts = sem("shift_order"), sem("shift_parts")
        shift_written = sem("shift_written")
        shift_loaded = [sem(f"shift_loaded{i}") for i in range(2)]
        s2_full, exp_done = sem("s2_full"), sem("exp_done")
        pv_done, oT_ready = sem("pv_done"), sem("oT_ready")
        sums_inv = sem("sums_inv")
        o_high = sem("o_high")
        tanh_ready, silu_ready = sem("tanh_ready"), sem("silu_ready")
        h_high, h_low = sem("h_high"), sem("h_low")
        down_done, x1_ready = sem("down_done"), sem("x1_ready")
        out_ready, out_stored = sem("out_ready"), sem("out_stored")

        raw = [E[:, 4 * i:4 * i + 4, :] for i in range(2)]
        RAW = [
            (w0.rearrange("w (c p) n -> p (w c) n", p=P), Wh[:, :, :, :].rearrange("p w c n -> p (w c n)"),
             Wl[:, :, :, :].rearrange("p w c n -> p (w c n)")),
        ] + [
            (w_ffn[i].rearrange("(c p) n -> p c n", p=P), Gh[:, i, :, :].rearrange("p c n -> p (c n)"),
             Gl[:, i, :, :].rearrange("p c n -> p (c n)")) for i in range(2)
        ] + [
            (w_out.rearrange("(c p) n -> p c n", p=P), Uh[:, :, :].rearrange("p c n -> p (c n)"),
             Ul[:, :, :].rearrange("p c n -> p (c n)")),
        ]
        SWAPS = {13: [0, 1], 14: [2], 16: [3]}

        def flat(ap):
            return ap.rearrange("p a b -> p (a b)")

        block = ctx.enter_context(nc.Block())

        @block.sync
        def _(sp):
            def load_x(n):
                sp.dma_start(X[:, bass.ds(n, 1), :, :].rearrange("p o c t -> p (o c) t"),
                             xT[:, :, bass.ds(n * T, T)].rearrange("c p t -> p c t")).then_inc(x_loaded, 16)

            load_x(0)
            for i, (src, _, _) in enumerate(RAW):
                if i >= 2:
                    after(sp, raw_lo, i - 1)
                sp.dma_start(raw[i % 2].rearrange("p a b -> p (a b)").rearrange(
                    "p (c n) -> p c n", c=src.shape[1]), src).then_inc(raw_loaded[i % 2], 16)
                if i == 1:
                    for dst, s in ((cT[:, 0, :], condT), (cb[:, :], cond_b), (rs[:, :], rms_scale)):
                        sp.dma_start(dst, s).then_inc(small_loaded, 16)
                    sp.dma_start(y[0:DT, :, :].rearrange("p a b -> p (a b)"), cond_w[:, 0:512]).then_inc(small_loaded, 16)
                    sp.dma_start(rest[0:DT, :, :].rearrange("p a b -> p (a b)"), cond_w[:, 512:1024]).then_inc(small_loaded, 16)
                    sp.dma_start(crm[0:DT, :, :].rearrange("p a b -> p (a b)"), cond_w[:, 1024:1536]).then_inc(small_loaded, 16)
                    sp.dma_start(hf[:, 0, 0:P].bitcast(I32).rearrange("p (c t) -> p c t", c=TC), mask).then_inc(small_loaded, 16)
                    sp.dma_start(hf[:, 1, 0:P].bitcast(I32).rearrange("p (c t) -> p c t", c=TC), maskT).then_inc(small_loaded, 16)

            def write_parts(scr, parts, written):
                for part in range(3):
                    for c in range(FC):
                        sp.dma_start(scr[8 * c:8 * c + 8, DH * part:DH * (part + 1), :],
                                     parts[:, part, c, :]).then_inc(written, 16)

            def read_stack(par, half_):
                hs = slice(8 * half_, 8 * half_ + 8)
                row = 0
                for parts in (3, 2, 1):
                    k = DH * parts
                    for dst, src in ((qst[par][row:row + k, hs, :], q_scr[par][hs, 0:k, :]),
                                     (kst[par][row:row + k, hs, :], k_scr[par][hs, 3 * DH - k:3 * DH, :])):
                        sp.dma_start(dst, src.rearrange("h r t -> r h t")).then_inc(stack_loaded[half_], 16)
                    row += k

            def step(st):
                L, par = st.L, st.par

                registers = []

                def held(count):
                    if isinstance(count, int):
                        return count
                    registers.append(nc.sync.alloc_register(f"held{st.s0}_{len(registers)}"))
                    nc.sync.reg_mov(registers[-1], count)
                    return nc.sync.snap(registers[-1], min_val=0, max_val=1 << 20)

                n_x, n_a, n_b1, n_b2 = st.n(3), st.n(2), st.n(1), st.n(0)
                x_before = held(16 * n_x)
                scratch_read = held(96 * (n_a - 1))
                a_split = held(n_a + 1)
                a_written = held(96 * (n_a + 1))
                heads_used = [held(UNITS * n_b2 + 8), held(UNITS * n_b2 + 16)]
                rows_used = held(UNITS * n_b2)
                rows_read = held(16 * n_b1)
                rows_written = [held(16 * (2 * n_b1 + 1)), held(16 * (2 * n_b1 + 2))]
                rows_made = [None, None]
                if L["B1"] is not None:
                    for half_ in range(2):
                        b, k = st.bank(f"sh{half_}")
                        rows_made[half_] = (work_free[b], held(k + 1))
                result_made = held(st.n(-1 - B) + 1)

                def shift_rows(half_):
                    after(sp, shift_loaded[half_], rows_read)
                    after(sp, *rows_made[half_])
                    sp.dma_start(m_scr[half_], nT[:, :]).then_inc(shift_written, 16)
                    if L["B2"] is not None:
                        after(sp, s2_full, rows_used)
                    after(sp, shift_written, rows_written[half_])
                    sp.dma_start(qst[1 - par][PARTS:ROWS, 8 * half_:8 * half_ + 8, :],
                                 m_scr[half_].rearrange("(r h) t -> r h t", r=3)).then_inc(shift_loaded[half_], 16)

                if L["N"] == 0 and st.s0 > FIRST:
                    after(sp, x_loaded, x_before)
                    load_x(n_x)
                if L["A"] is not None:
                    for half_ in range(2):
                        after(sp, stack_loaded[half_], scratch_read)
                    after(sp, q_low, a_split)
                    write_parts(q_scr[par], qp, q_written)
                    after(sp, k_low, a_split)
                    write_parts(k_scr[par], kp, k_written)
                if L["B1"] is not None:
                    shift_rows(0)
                if L["A"] is not None:
                    after(sp, q_written, a_written)
                    after(sp, k_written, a_written)
                    if L["B2"] is not None:
                        after(sp, s2_full, heads_used[0])
                    read_stack(par, 0)
                if L["B1"] is not None:
                    shift_rows(1)
                if L["A"] is not None:
                    if L["B2"] is not None:
                        after(sp, s2_full, heads_used[1])
                    read_stack(par, 1)
                for m in SWAPS.get(st.s0, ()):
                    after(sp, swap_lo, m)
                    if m == 0:
                        sp.wait_ge(n_lo, B)
                        sp.wait_ge(n_hi, B)
                    sp.dma_start(nrm[:, :, :], w1[m].rearrange("(c p) n -> p c n", p=P)).then_inc(swap_loaded, 16)
                if L["C"] == 1:
                    n = st.n(-1 - B)
                    after(sp, out_ready, result_made)
                    sp.dma_start(yT[:, :, bass.ds(n * T, T)].rearrange("c p t -> p c t"), crm[:, :, :])\
                      .then_inc(out_stored, 16)
                for r in registers:
                    nc.sync.free_register(r)

            run_steps(nc.sync, step)
            sp.wait_ge(out_stored, 16 * B)

        @block.tensor
        def _(pe):
            mm = nc.tensor.matmul

            def mm3(out, lh, ll, rh, rl, first, last):
                mm(out, lh, rh, start=first, stop=False, skip_group_check=True)
                mm(out, lh, rl, start=False, stop=False, skip_group_check=True)
                return mm(out, ll, rh, start=False, stop=last, skip_group_check=True)

            pe.wait_ge(small_loaded, 16 * 8)
            pe.wait_ge(cond_silu, 1)
            for c in range(CCH):
                src = (y, rest, crm)[c // 4][0:DT, :, :].rearrange("p a b -> p (a b)")
                last = mm(acc[:, B * c:B * (c + 1)], src[:, P * (c % 4):P * (c % 4 + 1)],
                          cT[:, 0 if c < 8 else 1, :], start=True, stop=True)
            last.then_inc(cond_mm, 1)
            pe.wait_ge(consts, 5)
            pe.wait_ge(stack_ones, 2)

            def open_bank(st, use):
                b, k = st.bank(use)
                after(pe, work_free[b], k)
                return work[b], work_full[b]

            def project_T(out, w, xh, xl, chunks=FC):
                for m in range(FC):
                    for c in range(chunks):
                        last = mm3(out[:, m * T:(m + 1) * T], Wh[:, w, c, P * m:P * (m + 1)],
                                   Wl[:, w, c, P * m:P * (m + 1)], xh[:, c, :], xl[:, c, :],
                                   c == 0, c == chunks - 1)
                return last

            def scores_for_max(st, g):
                n, par = st.n(1), 1 - st.par
                if g in (0, 4):
                    after(pe, stack_loaded[g // 4], 96 * (n + 1))
                for qh in range(TC):
                    u = 2 * g + qh
                    after(pe, s1_free, UNITS * n + u - 1)
                    bank = s1ps[u % 2]
                    if st.L["B1"] == 1:
                        mm(bank[:, :].rearrange("p (h t) -> p h t", h=2), identb[:, :],
                           msk[:, qh, :][:, None, :].to_broadcast([P, 2, T]),
                           start=True, stop=False, skip_group_check=True)
                    for i in range(2):
                        h = 2 * g + i
                        last = mm(bank[:, T * i:T * (i + 1)], qst[par][0:PARTS, h, P * qh:P * (qh + 1)],
                                  kst[par][0:PARTS, h, :], start=st.L["B1"] == 0, stop=True,
                                  skip_group_check=True)
                    last.then_inc(s1_full, 1)

            def scores(st, g):
                n, par = st.n(0), st.par
                if g in (0, 4):
                    after(pe, shift_loaded[g // 4], 16 * (n + 1))
                for kh in range(TC):
                    u = 2 * g + kh
                    after(pe, exp_done, UNITS * n + u - 1)
                    bank = s2ps[u % 2]
                    if st.L["B2"] == 1:
                        mm(bank[:, :].rearrange("p (h t) -> p h t", h=2), identb[:, :],
                           mskT[:, kh, :][:, None, :].to_broadcast([P, 2, T]),
                           start=True, stop=False, skip_group_check=True)
                    for i in range(2):
                        h = 2 * g + i
                        last = mm(bank[:, T * i:T * (i + 1)], kst[par][0:ROWS, h, P * kh:P * (kh + 1)],
                                  qst[par][0:ROWS, h, :], start=st.L["B2"] == 0, stop=True,
                                  skip_group_check=True)
                    last.then_inc(s2_full, 1)

            def values(st, j):
                n = st.n(0)
                after(pe, exp_done, UNITS * n + 4 * j + 4)
                if j % 2 == 0:
                    after(pe, oT_ready, 2 * n + j // 2)
                for kh in range(TC):
                    for i in range(4):
                        h = 4 * j + i
                        u = 2 * (h // 2) + kh
                        last = mm(pvps[32 * i:32 * (i + 1), T * (j % 2):T * (j % 2 + 1)],
                                  vaug[st.par][:, kh, h, :], E[:, u % E_RING, T * (h % 2):T * (h % 2 + 1)],
                                  start=kh == 0, stop=kh == TC - 1, skip_group_check=True)
                last.then_inc(pv_done, 1)

            def swiglu_up(st, i):
                bank, full = open_bank(st, f"F{i}")
                if i == 0:
                    after(pe, c_lo, st.n(-2) + 1)
                for w in range(2):
                    for c in range(FC):
                        last = mm3(bank[:, T * w:T * (w + 1)], Gh[:, w, c, P * i:P * (i + 1)],
                                   Gl[:, w, c, P * i:P * (i + 1)], xch[st.par][:, c, :],
                                   xcl[st.par][:, c, :], c == 0, c == FC - 1)
                last.then_inc(full, 1)

            def swiglu_down(st, i):
                n = st.n(-2)
                after(pe, h_low, HC * n + i + 1)
                if i == 0:
                    after(pe, x1_ready, n)
                for m in range(FC):
                    last = mm3(acc[:, T * m:T * (m + 1)], Uh[:, i, P * m:P * (m + 1)],
                               Ul[:, i, P * m:P * (m + 1)], hh[:, i % 2, :], hl[:, i % 2, :],
                               i == 0 and m == 0, i == HC - 1)
                last.then_inc(down_done, 1)

            def divide_in(st):
                after(pe, oT_ready, 2 * st.n(-1) + 2)
                for qh, use in enumerate(("T1a", "T1b")):
                    bank, full = open_bank(st, use)
                    for j in range(4):
                        last = nc.tensor.transpose(bank[:, P * j:P * (j + 1)], oT[:, j, P * qh:P * (qh + 1)],
                                                   ident[:, :])
                    last.then_inc(full, 1)

            def divide_out(st):
                for use in ("T1a", "T1b"):
                    b, k = st.bank(use)
                    after(pe, work_free[b], k + 1)
                bank, full = open_bank(st, "T2")
                for m in range(FC):
                    for qh in range(TC):
                        src = on[:, qh, 8 * m:8 * m + 8, :].rearrange("p h d -> p (h d)")
                        last = nc.tensor.transpose(bank[:, T * m + P * qh:T * m + P * (qh + 1)], src,
                                                   ident[:, :])
                last.then_inc(full, 1)

            def value_projection(st):
                n = st.n(1)
                par = 1 - st.par
                after(pe, n_lo, n + 1)
                bank, full = open_bank(st, "V")
                for t in range(TC):
                    for c in range(FC):
                        last = mm3(bank[:, D * t:D * (t + 1)], xnh[par][:, c, P * t:P * (t + 1)],
                                   xnl[par][:, c, P * t:P * (t + 1)], Wh[:, 2, c, :], Wl[:, 2, c, :],
                                   c == 0, c == FC - 1)
                last.then_inc(full, 1)

            def output_projection(st):
                b, k = st.bank("T2")
                after(pe, work_free[b], k + 1)
                bank, full = open_bank(st, "Wo")
                project_T(bank, 3, oh, ol).then_inc(full, 1)

            def qk_projection(st, use, w):
                after(pe, n_lo, st.n(2) + 1)
                bank, full = open_bank(st, use)
                project_T(bank, w, xnh[st.par], xnl[st.par]).then_inc(full, 1)

            def mean_squares(st):
                bank, full = open_bank(st, "ms")
                jobs = []
                if st.L["N"] == 0:
                    after(pe, sq_n, st.n(3) + 1)
                    jobs.append((nrm[:, :, :], 0))
                if st.L["C"] is not None:
                    after(pe, sq_c, st.n(-1) + 1)
                    jobs.append((dg[:, :, :].rearrange("p (c u) t -> p c (u t)", c=FC), 2))
                for src, col in jobs:
                    for t in range(TC):
                        for c in range(FC):
                            last = mm(bank[:, col + t:col + t + 1], src[:, c, P * t:P * (t + 1)],
                                      mean1[:, :], start=c == 0, stop=c == FC - 1, skip_group_check=True)
                last.then_inc(full, 1)

            def broadcast_rstd(st, use, col):
                bank, full = open_bank(st, use)
                after(pe, diag_ready, st.n(3) + 1)
                mm(bank[:, 0:T], ones[:, :], dg[:, col:col + 2, :].rearrange("p a b -> p (a b)"),
                   start=True, stop=True).then_inc(full, 1)

            def shift_transpose(st, half_):
                bank, full = open_bank(st, f"sh{half_}")
                after(pe, shift_parts, 2 * st.n(1) + half_ + 1)
                out = bank[0:24, 0:P].bitcast(BF16)
                for qh in range(TC):
                    last = nc.tensor.transpose(out[:, P * qh:P * (qh + 1)],
                                               nparts[:, qh, :, :].rearrange("p r h -> p (r h)"), identb[:, :])
                last.then_inc(full, 1)

            def step(st):
                L = st.L
                if st.s0 == FIRST:
                    pe.wait_ge(raw_lo, 4)
                if st.s0 == B - 1:
                    pe.wait_ge(masks_ready, 2)
                for g in range(SLOTS):
                    if L["B1"] is not None:
                        scores_for_max(st, g)
                    if L["B2"] is not None:
                        scores(st, g)
                        if g in (2, 4, 6):
                            values(st, g // 2 - 1)
                    if L["C2"] is not None:
                        swiglu_up(st, g)
                        if g >= 2:
                            swiglu_down(st, g - 2)
                    if g == 0 and L["C"] is not None:
                        divide_in(st)
                    if g == 1:
                        if L["C"] is not None:
                            divide_out(st)
                        if L["V"] is not None:
                            if st.s0 + 1 == B:
                                pe.wait_ge(swap_lo, 3)
                            value_projection(st)
                    if g == 2:
                        if L["C"] is not None:
                            if st.s0 - 1 == B:
                                pe.wait_ge(swap_lo, 4)
                            output_projection(st)
                        if L["A"] is not None:
                            if st.s0 + 2 == B:
                                pe.wait_ge(swap_lo, 2)
                            qk_projection(st, "Q", 0)
                    if g == 3 and L["A"] is not None:
                        qk_projection(st, "K", 1)
                    if g == 4:
                        if L["N"] == 0 or L["C"] is not None:
                            mean_squares(st)
                        if L["B1"] is not None:
                            shift_transpose(st, 0)
                    if g == 6:
                        if L["N"] == 0:
                            broadcast_rstd(st, "bcN", 0)
                        if L["C"] is not None:
                            broadcast_rstd(st, "bcC", 2)
                if L["B2"] is not None:
                    values(st, 3)
                if L["C2"] is not None:
                    swiglu_down(st, 6)
                    swiglu_down(st, 7)
                if L["B1"] is not None:
                    shift_transpose(st, 1)

            run_steps(nc.tensor, step)

        @block.vector
        def _(dve):
            v = nc.vector
            for i in range(2):
                v.memset(kst[i][PARTS:ROWS, :, :], 1.0).then_inc(stack_ones, 1)
            for i, (_, hi, lo) in enumerate(RAW):
                dve.wait_ge(raw_loaded[i % 2], 16 * (i // 2 + 1))
                dve.wait_ge(raw_hi, i + 1)
                v.tensor_tensor(lo, flat(raw[i % 2]), hi.bitcast(F32), ALU.subtract).then_inc(raw_lo, 1)
                if i == 0:
                    dve.wait_ge(cond_tanh, 1)
                    v.tensor_scalar(cth[:, :], cth[:, :], 0.5, 0.5, ALU.mult, ALU.add).then_inc(setup, 1)
                    dve.wait_ge(setup, 1)
                    v.tensor_tensor(cT[:, 1, :], cth[:, :], cT[:, 0, :], ALU.mult).then_inc(cond_silu, 1)
                    v.tensor_scalar(msk[:, :, :], hf[:, 0, 0:P].bitcast(U8).rearrange("p (c t) -> p c t", c=TC),
                                    NEG, None, ALU.mult).then_inc(masks_ready, 1)
                    v.tensor_scalar(mskT[:, :, :], hf[:, 1, 0:P].bitcast(U8).rearrange("p (c t) -> p c t", c=TC),
                                    NEG, None, ALU.mult).then_inc(masks_ready, 1)
                    dve.wait_ge(cond_mm, 1)
                    v.tensor_tensor(cond[:, :, :], acc[:, 0:CCH * B].rearrange("p (c b) -> p c b", c=CCH),
                                    cb[:, :][:, :, None].to_broadcast([P, CCH, B]), ALU.add).then_inc(setup, 1)
                    dve.wait_ge(setup, 2)
                    for c in range(FC):
                        v.tensor_scalar(cond[:, C_SCALE + c, :], cond[:, C_SCALE + c, :], 1.0,
                                        rs[:, c:c + 1], ALU.add, ALU.mult).then_inc(cond_ready, 1)
            dve.wait_ge(consts, 5)

            def maxima(st, g):
                n = st.n(1)
                for qh in range(TC):
                    u = 2 * g + qh
                    after(dve, s1_full, UNITS * n + u + 1)
                    v.tensor_reduce(nmax[:, g // 4, qh, 2 * (g % 4):2 * (g % 4) + 2],
                                    s1ps[u % 2][:, :].rearrange("p (h t) -> p h t", h=2), AX_X, ALU.max,
                                    negate=True).then_inc(s1_free, 1)

            def shift_split(st, half_):
                n = st.n(1)
                k = 2 * n + half_
                done = SHIFT_OPS * k
                nm = nmax[:, half_, :, :]
                after(dve, s1_free, UNITS * n + 8 * half_ + 8)
                v.tensor_scalar(nm, nm, CLAMP, None, ALU.min).then_inc(shift_order, 1)
                after(dve, shift_order, done + 1)
                if half_ or st.s0 >= 0:
                    b, k = st.bank("sh0") if half_ else st.last().bank("sh1")
                    after(dve, work_full[b], k + 1)
                v.tensor_copy(nparts[:, :, 0, :], nm).then_inc(shift_order, 1)
                after(dve, shift_order, done + 2)
                v.tensor_tensor(nrest[:, :, :], nm, nparts[:, :, 0, :], ALU.subtract).then_inc(shift_order, 1)
                after(dve, shift_order, done + 3)
                v.tensor_copy(nparts[:, :, 1, :], nrest[:, :, :]).then_inc(shift_order, 1)
                after(dve, shift_order, done + 4)
                v.tensor_tensor(nparts[:, :, 2, :], nrest[:, :, :], nparts[:, :, 1, :],
                                ALU.subtract).then_inc(shift_parts, 1)

            def opened(st, use):
                b, k = st.bank(use)
                after(dve, work_full[b], k + 1)
                return work[b], work_free[b]

            def divide(st):
                for qh, use in enumerate(("T1a", "T1b")):
                    bank, free = opened(st, use)
                    heads = bank[:, :].rearrange("p (h w) -> p h w", w=VW)
                    v.reciprocal(rsum[:, qh, :], heads[:, :, DH]).then_inc(sums_inv, 1)
                    after(dve, sums_inv, TC * st.n(-1) + qh + 1)
                    v.tensor_tensor(on[:, qh, :, :], heads[:, :, 0:DH],
                                    rsum[:, qh, :][:, :, None].to_broadcast([P, H, DH]), ALU.mult)\
                     .then_inc(free, 1)

            def o_split(st):
                bank, free = opened(st, "T2")
                after(dve, o_high, st.n(-1) + 1)
                v.tensor_tensor(flat(ol[:, :, :]), bank[:, :], flat(oh[:, :, :]).bitcast(F32), ALU.subtract)\
                 .then_inc(free, 1)

            def qk_split(st, use, parts, hi_at, high, mid, low):
                n = st.n(2)
                bank, free = opened(st, use)
                after(dve, high, n + 1)
                after(dve, k_low if use == "Q" else q_low, n if use == "Q" else n + 1)
                v.tensor_tensor(flat(rest[:, :, :]), bank[:, :],
                                parts[:, hi_at, :, :].rearrange("p c t -> p (c t)"), ALU.subtract).then_inc(free, 1)
                b, k = st.bank(use)
                after(dve, work_free[b], k + 1)
                v.tensor_copy(parts[:, 1, :, :], rest[:, :, :]).then_inc(mid, 1)

            def attention_residual(st):
                n = st.n(-1)
                bank, free = opened(st, "Wo")
                after(dve, z_ready, n)
                v.tensor_tensor(flat(y[:, :, :]), bank[:, :],
                                X[:, bass.ds(n, 1), :, :].rearrange("p o c t -> p (o c t)"), ALU.add)\
                 .then_inc(free, 1)

            def rsqrt(st):
                lo = 0 if st.L["N"] == 0 else 2
                hi = 4 if st.L["C"] is not None else 2
                c = slice(lo, hi)
                done = NEWTON_OPS * st.n(3)
                bank, free = opened(st, "ms")
                v.tensor_scalar(var[:, c], bank[:, c], EPS, None, ALU.add).then_inc(free, 1)
                b, k = st.bank("ms")
                after(dve, work_free[b], k + 1)
                v.tensor_scalar(half[:, c].bitcast(I32), var[:, c].bitcast(I32), 1, None,
                                ALU.logical_shift_right).then_inc(newton, 1)
                after(dve, newton, done + 1)
                v.tensor_scalar(rstd[:, c].bitcast(I32), half[:, c].bitcast(I32), -1.0, RSQRT_MAGIC,
                                ALU.mult, ALU.add).then_inc(newton, 1)
                for i in range(3):
                    after(dve, newton, done + 3 * i + 2)
                    v.tensor_tensor(tmp4[:, c], rstd[:, c], rstd[:, c], ALU.mult).then_inc(newton, 1)
                    after(dve, newton, done + 3 * i + 3)
                    v.scalar_tensor_tensor(tmp4[:, c], tmp4[:, c], -0.5, var[:, c], ALU.mult, ALU.mult)\
                     .then_inc(newton, 1)
                    after(dve, newton, done + 3 * i + 4)
                    v.scalar_tensor_tensor(rstd[:, c], tmp4[:, c], 1.5, rstd[:, c], ALU.add, ALU.mult)\
                     .then_inc(newton, 1)
                after(dve, newton, done + NEWTON_OPS)
                v.tensor_tensor(dg[:, c, :], ident[:, :][:, None, :].to_broadcast([P, hi - lo, P]),
                                rstd[:, c][:, :, None].to_broadcast([P, hi - lo, P]), ALU.mult)\
                 .then_inc(diag_ready, 1)

            def normalize(st, use, dst, src):
                bank, free = opened(st, use)
                v.tensor_tensor(dst, src, bank[:, 0:T][:, None, :].to_broadcast([P, FC, T]), ALU.mult)\
                 .then_inc(free, 1)

            def swiglu(st, i):
                n = st.n(-2)
                bank, free = opened(st, f"F{i}")
                after(dve, tanh_ready, HC * n + i + 1)
                v.scalar_tensor_tensor(th[:, i % 2, :], th[:, i % 2, :], 1.0, bank[:, 0:T],
                                       ALU.add, ALU.mult).then_inc(silu_ready, 1)
                after(dve, silu_ready, HC * n + i + 1)
                after(dve, h_low, HC * n + i - 1)
                v.scalar_tensor_tensor(hf[:, i % 2, :], th[:, i % 2, :], 0.5, bank[:, T:2 * T],
                                       ALU.mult, ALU.mult).then_inc(free, 1)

            def step(st):
                L = st.L
                for g in range(SLOTS):
                    if L["B1"] is not None:
                        maxima(st, g)
                    if L["C2"] is not None:
                        swiglu(st, g)
                    if g == 0 and L["C"] is not None:
                        divide(st)
                    if g == 1 and L["C"] is not None:
                        o_split(st)
                    if g == 2:
                        if L["C"] == 0:
                            attention_residual(st)
                        if L["A"] is not None:
                            qk_split(st, "Q", qp, 0, q_high, q_mid, q_low)
                    if g == 3:
                        if L["A"] is not None:
                            qk_split(st, "K", kp, 2, k_high, k_mid, k_low)
                        if L["B1"] is not None:
                            shift_split(st, 0)
                    if g == 4 and (L["N"] == 0 or L["C"] is not None):
                        rsqrt(st)
                    if g == 6:
                        if L["N"] == 0:
                            n = st.n(3)
                            normalize(st, "bcN", nrm[:, :, :],
                                      X[:, bass.ds(n, 1), :, :].rearrange("p o c t -> p (o c) t"))
                        if L["C"] is not None:
                            if L["C"] == 1:
                                after(dve, out_stored, 16 * (st.n(-1) - B))
                            normalize(st, "bcC", crm[:, :, :], y[:, :, :])
                if L["B1"] is not None:
                    shift_split(st, 1)
                if L["C2"] is not None:
                    n = st.n(-2)
                    after(dve, down_done, HC * (n + 1))
                    xb = X[:, bass.ds(n, 1), :, :].rearrange("p o c t -> p (o c t)")
                    v.tensor_tensor(xb, acc[:, :], xb, ALU.add).then_inc(x1_ready, 1)
                for m in SWAPS.get(st.s0, ()):
                    dve.wait_ge(swap_hi, m + 1)
                    v.tensor_tensor(Wl[:, m, :, :], nrm[:, :, :], Wh[:, m, :, :].bitcast(F32),
                                    ALU.subtract).then_inc(swap_lo, 1)

            run_steps(nc.vector, step)

        @block.scalar
        def _(act):
            a = nc.scalar
            for i, (_, hi, lo) in enumerate(RAW):
                act.wait_ge(raw_loaded[i % 2], 16 * (i // 2 + 1))
                a.copy(hi, flat(raw[i % 2])).then_inc(raw_hi, 1)
                if i == 0:
                    act.wait_ge(small_loaded, 16 * 8)
                    a.activation(cth[:, :], cT[:, 0, :], ACT.Tanh, scale=0.5).then_inc(cond_tanh, 1)
            act.wait_ge(cond_ready, 2)

            def opened(st, use):
                b, k = st.bank(use)
                after(act, work_full[b], k + 1)
                return work[b], work_free[b]

            def exps(st, g):
                n = st.n(0)
                for kh in range(TC):
                    u = 2 * g + kh
                    after(act, s2_full, UNITS * n + u + 1)
                    after(act, pv_done, 4 * n + u // 4 - 1)
                    a.activation(E[:, u % E_RING, :], s2ps[u % 2][:, :], ACT.Exp, scale=SCORE_SCALE)\
                     .then_inc(exp_done, 1)

            def store_oT(st, pair):
                n = st.n(0)
                after(act, pv_done, 4 * n + 2 * pair + 2)
                if pair == 0 and st.L["C"] is not None:
                    for use in ("T1a", "T1b"):
                        b, k = st.bank(use)
                        after(act, work_full[b], k + 1)
                a.copy(oT[:, 2 * pair:2 * pair + 2, :], pvps[:, :].rearrange("p (j t) -> p j t", j=2))\
                 .then_inc(oT_ready, 1)

            def tanh(st, i):
                bank, _ = opened(st, f"F{i}")
                if i >= 2:
                    b, k = st.bank(f"F{i - 2}")
                    after(act, work_free[b], k + 1)
                a.activation(th[:, i % 2, :], bank[:, 0:T], ACT.Tanh, scale=0.5).then_inc(tanh_ready, 1)

            def h_high_part(st, i):
                n = st.n(-2)
                b, k = st.bank(f"F{i}")
                after(act, work_free[b], k + 1)
                after(act, down_done, HC * n + i - 1)
                a.copy(hh[:, i % 2, :], hf[:, i % 2, :]).then_inc(h_high, 1)

            def affine(st, buf, gain, shift, b, done, count):
                for c in range(FC):
                    a.activation(buf[:, c, :], buf[:, c, :], ACT.Identity,
                                 scale=cond[:, gain + c, bass.ds(b, 1)],
                                 bias=cond[:, shift + c, bass.ds(b, 1)]).then_inc(done, 1)
                after(act, done, count)

            def step(st):
                L = st.L
                for g in range(SLOTS):
                    if L["B2"] is not None:
                        exps(st, g)
                    if L["C2"] is not None:
                        tanh(st, g)
                        if g >= 1:
                            h_high_part(st, g - 1)
                    if g == 1:
                        if L["C"] is not None:
                            bank, _ = opened(st, "T2")
                            a.copy(flat(oh[:, :, :]), bank[:, :]).then_inc(o_high, 1)
                        if L["V"] is not None:
                            bank, free = opened(st, "V")
                            after(act, pv_done, 4 * st.n(0))
                            a.copy(vaug[1 - st.par][:, :, :, 0:DH],
                                   bank[:, :].rearrange("p (t h d) -> p t h d", t=TC, h=H)).then_inc(free, 1)
                    if g == 2:
                        if L["C"] == 1:
                            bank, free = opened(st, "Wo")
                            b, k = st.last().bank("bcC")
                            after(act, work_free[b], k + 1)
                            if st.s0 - 1 == B:
                                act.wait_ge(z_ready, B)
                            a.copy(flat(y[:, :, :]), bank[:, :]).then_inc(free, 1)
                        if L["A"] is not None:
                            bank, _ = opened(st, "Q")
                            after(act, q_written, 96 * st.n(2))
                            a.copy(qp[:, 0, :, :].rearrange("p c t -> p (c t)"), bank[:, :]).then_inc(q_high, 1)
                    if g == 3 and L["A"] is not None:
                        bank, _ = opened(st, "K")
                        after(act, k_written, 96 * st.n(2))
                        a.copy(kp[:, 2, :, :].rearrange("p c t -> p (c t)"), bank[:, :]).then_inc(k_high, 1)
                    if g == 5:
                        if L["B2"] is not None:
                            store_oT(st, 0)
                        if L["B1"] is not None:
                            shift_store(st, 0)
                    if g == 7:
                        if L["N"] == 0:
                            n = st.n(3)
                            b, k = st.bank("bcN")
                            after(act, work_free[b], k + 1)
                            affine(st, nrm, C_G1, C_B1, n, n_affine, 2 * (n + 1))
                            a.copy(xnh[1 - st.par][:, :, :], nrm[:, :, :]).then_inc(n_hi, 1)
                        if L["C"] is not None:
                            n = st.n(-1)
                            b, k = st.bank("bcC")
                            after(act, work_free[b], k + 1)
                            if L["C"] == 0:
                                affine(st, crm, C_G2, C_B2, n, c_affine, 2 * (n + 1))
                                a.copy(xch[1 - st.par][:, :, :], crm[:, :, :]).then_inc(c_hi, 1)
                            else:
                                affine(st, crm, C_SCALE, C_SHIFT, n - B, c_affine, 2 * (n + 1))
                    if g == 3 and L["N"] == 1:
                        n = st.n(3)
                        after(act, x1_ready, n - B + 1)
                        a.copy(xnh[1 - st.par][:, :, :],
                               X[:, bass.ds(n - B, 1), :, :].rearrange("p o c t -> p (o c) t")).then_inc(n_hi, 1)
                if L["C2"] is not None:
                    h_high_part(st, 7)
                if L["B2"] is not None:
                    store_oT(st, 1)
                if L["B1"] is not None:
                    shift_store(st, 1)
                for m in SWAPS.get(st.s0, ()):
                    act.wait_ge(swap_loaded, 16 * (m + 1))
                    if m == 0:
                        b, k = st.bank("K")
                        act.wait_ge(work_full[b], k + 1)
                    if m == 2:
                        b, k = st.bank("V")
                        act.wait_ge(work_full[b], k + 1)
                    if m == 3:
                        b, k = st.bank("Wo")
                        act.wait_ge(work_full[b], k + 1)
                    a.copy(Wh[:, m, :, :], nrm[:, :, :]).then_inc(swap_hi, 1)

            def shift_store(st, half_):
                bank, free = opened(st, f"sh{half_}")
                after(act, shift_written, 16 * (2 * st.n(1) + half_))
                a.copy(nT[:, :], bank[0:24, 0:P].bitcast(BF16)).then_inc(free, 1)

            run_steps(nc.scalar, step)

        @block.gpsimd
        def _(pool):
            p = nc.gpsimd
            p.memset(ident[:, :], 0.0).then_inc(consts, 1)
            p.memset(ones[:, :], 1.0)
            p.memset(mean1[:, :], 1.0 / D)
            for i in range(2):
                last = p.memset(vaug[i][:, :, :, DH:VW], 0.0)
            last.then_inc(consts, 1)
            pool.wait_ge(consts, 2)
            p.affine_select(out=ident[:, :], in_=ident[:, :], compare_op=ALU.not_equal, fill=1.0, base=0,
                            pattern=[[-1, P]], channel_multiplier=1).then_inc(consts, 1)
            pool.wait_ge(consts, 3)
            p.tensor_copy(identb[:, :], ident[:, :]).then_inc(consts, 1)
            for i in range(2):
                last = p.memset(vaug[i][:, :, :, DH:DH + 1], 1.0)
            last.then_inc(consts, 1)

            def xb(n):
                return X[:, bass.ds(n, 1), :, :].rearrange("p o c t -> p (o c) t")

            def low_q(st, parts, hi_at, lo_at, mid, low):
                n = st.n(2)
                after(pool, mid, n + 1)
                p.tensor_tensor(parts[:, lo_at, :, :], rest[:, :, :], parts[:, 1, :, :],
                                ALU.subtract).then_inc(low, 1)

            def step(st):
                L = st.L
                for g in range(SLOTS):
                    if L["C2"] is not None and g >= 1:
                        h_low_part(st, g - 1)
                    if g == 2:
                        if L["C"] is not None:
                            n = st.n(-1)
                            b, k = st.bank("Wo")
                            after(pool, work_free[b], k + 1)
                            b, k = st.last().bank("bcC" if st.s0 >= 2 else "bcN")
                            after(pool, work_full[b], k + 1)
                            p.tensor_tensor(dg[:, :, :].rearrange("p (c u) t -> p c (u t)", c=FC),
                                            y[:, :, :], y[:, :, :], ALU.mult).then_inc(sq_c, 1)
                            if L["C"] == 0:
                                p.tensor_tensor(xb(n), xb(n), y[:, :, :], ALU.add).then_inc(z_ready, 1)
                        if L["A"] is not None:
                            low_q(st, qp, 0, 2, q_mid, q_low)
                    if g == 2 and L["N"] == 0:
                        n = st.n(3)
                        after(pool, x_loaded, 16 * (n + 1))
                        after(pool, n_hi, n)
                        p.tensor_tensor(nrm[:, :, :], xb(n), xb(n), ALU.mult).then_inc(sq_n, 1)
                    if g == 3:
                        if L["A"] is not None:
                            low_q(st, kp, 2, 0, k_mid, k_low)
                        if L["N"] == 1:
                            n = st.n(3)
                            after(pool, n_hi, n + 1)
                            b, k = st.bank("V") if L["V"] is not None else (0, -1)
                            after(pool, work_full[b], k + 1)
                            p.tensor_tensor(xnl[1 - st.par][:, :, :], xb(n - B),
                                            xnh[1 - st.par][:, :, :].bitcast(F32), ALU.subtract).then_inc(n_lo, 1)
                if L["N"] == 0:
                    after(pool, n_hi, st.n(3) + 1)
                    p.tensor_tensor(xnl[1 - st.par][:, :, :], nrm[:, :, :],
                                    xnh[1 - st.par][:, :, :].bitcast(F32), ALU.subtract).then_inc(n_lo, 1)
                if L["C"] == 0:
                    after(pool, c_hi, st.n(-1) + 1)
                    p.tensor_tensor(xcl[1 - st.par][:, :, :], crm[:, :, :],
                                    xch[1 - st.par][:, :, :].bitcast(F32), ALU.subtract).then_inc(c_lo, 1)
                if L["C"] == 1:
                    n = st.n(-1)
                    after(pool, c_affine, 2 * (n + 1))
                    p.tensor_tensor(crm[:, :, :], crm[:, :, :], xb(n - B), ALU.add).then_inc(out_ready, 1)
                if L["C2"] is not None:
                    h_low_part(st, 7)

            def h_low_part(st, i):
                n = st.n(-2)
                after(pool, h_high, HC * n + i + 1)
                after(pool, down_done, HC * n + i - 1)
                p.tensor_tensor(hl[:, i % 2, :], hf[:, i % 2, :], hh[:, i % 2, :].bitcast(F32),
                                ALU.subtract).then_inc(h_low, 1)

            run_steps(nc.gpsimd, step)


def kernel(**inputs):
    import numpy as np
    import concourse.bacc as bacc
    from concourse.bass_utils import run_bass_kernel_spmd

    a = {k: np.asarray(v) for k, v in inputs.items()}

    def t(name):
        return a[name].T

    def chunks(vec):
        return vec.reshape(-1, P).T

    def words(m):
        return np.ascontiguousarray(m).view(np.int32).reshape(TC, P, T // 4).transpose(1, 0, 2)

    arrays = {
        "xT": a["x"].transpose(2, 0, 1).reshape(FC, P, B * T),
        "w0": np.stack([t("L0_cond_Wq"), t("L0_cond_Wk"), t("L0_cond_Wv"), t("L0_cond_Wo")]),
        "w_ffn": np.stack([t("L0_cond_gate_w"), t("L0_cond_hid_w")]),
        "w_out": t("L0_cond_out_w"),
        "w1": np.stack([t("L1_cond_Wq"), t("L1_cond_Wk"), t("L1_cond_Wv"), t("L1_cond_Wo")]),
        "condT": t("cond_256"),
        "cond_w": np.concatenate([t("L0_cond_g1w"), t("L0_cond_b1w"), t("L0_cond_g2w"), t("L0_cond_b2w"),
                                  t("L1_cond_Wc")], axis=1),
        "cond_b": chunks(np.concatenate([a["L0_cond_g1b"], a["L0_cond_b1b"], a["L0_cond_g2b"],
                                         a["L0_cond_b2b"], a["L1_cond_bc"]])),
        "rms_scale": chunks(a["L1_cond_rms_scale"]),
        "mask": words(a["mask_SxS_bk1"]),
        "maskT": words(a["mask_SxS_bk1"].T),
    }
    arrays = {k: np.ascontiguousarray(v) for k, v in arrays.items()}
    nc = bacc.Bacc("TRN2", target_bir_lowering=False, num_devices=1)
    args = [nc.dram_tensor(k, v.shape, mybir.dt.from_np(v.dtype), kind="ExternalInput").ap()
            for k, v in arrays.items()]
    args.append(nc.dram_tensor("yT", (FC, P, B * T), F32, kind="ExternalOutput").ap())
    build(nc, *args)
    r = run_bass_kernel_spmd(nc, [arrays], core_ids=[0])
    out = np.asarray(r.results[0]["yT"])
    return np.ascontiguousarray(out.reshape(D, B, T).transpose(1, 2, 0))
```

```python
from contextlib import ExitStack

import concourse.bass as bass
from concourse import mybir

F32 = mybir.dt.float32
F32R = mybir.dt.float32r
BF16 = mybir.dt.bfloat16
I32 = mybir.dt.int32
U8 = mybir.dt.uint8
ACT = mybir.ActivationFunctionType
ALU = mybir.AluOpType
AX_X = mybir.AxisListType.X

P = 128
B = 16
T = 256
D = 256
H = 16
DH = D // H
HID = 1024
FC = D // P
TC = T // P
HC = HID // P
DT = 64
EPS = 1e-6
SCORE_SCALE = DH ** -0.5
PARTS = 6 * DH
ROWS = PARTS + 3
SLOTS = 8
UNITS = 16
E_RING = 8
VW = 32
NEG = -1.0e38
CLAMP = 5.0e37
RSQRT_MAGIC = float(0x5F3759DF)
NEWTON_OPS = 12
BRANCH = B - 1
SHIFT_OPS = 4
FIRST, LAST = -3, 2 * B

C_G1, C_B1, C_G2, C_B2, C_SHIFT, C_SCALE = 0, 2, 4, 6, 8, 10
CCH = 12


def stages(s):
    def layer(n):
        return None if n < 0 or n >= 2 * B else n // B
    at = {"N": s + 3, "A": s + 2, "V": s + 1, "B1": s + 1, "B2": s, "C": s - 1}
    found = {k: layer(n) for k, n in at.items()}
    found["C2"] = 0 if layer(s - 2) == 0 else None
    found["C3"] = 0 if layer(s - 3) == 0 else None
    return found


def bank_uses(L):
    uses = []
    for g in range(SLOTS):
        if g == 0 and L["C"] is not None:
            uses += ["T1a", "T1b"]
        if g == 1:
            uses += ["T2"] * (L["C"] is not None) + ["V"] * (L["V"] is not None)
        if g == 2:
            uses += ["Wo"] * (L["C"] is not None) + ["Q"] * (L["A"] is not None)
        if g == 3 and L["A"] is not None:
            uses.append("K")
        if g == 4:
            uses += ["ms"] * (L["N"] == 0 or L["C"] is not None) + ["sh0"] * (L["B1"] is not None)
        if g == 6:
            uses += ["bcC"] * (L["C"] is not None) + ["bcN"] * (L["N"] == 0)
        if L["C2"] is not None:
            uses.append(f"F{g}")
    return uses + ["sh1"] * (L["B1"] is not None)


USES_BEFORE = {FIRST: 0}
for _s in range(FIRST, LAST + 1):
    USES_BEFORE[_s + 1] = USES_BEFORE[_s] + len(bank_uses(stages(_s)))


class Step:

    def __init__(self, s0, turn=None, full=True):
        self.s0, self.turn, self.full = s0, turn, full
        self.par = s0 % 2
        self.L = stages(s0)
        self.s = s0 if turn is None else turn * 2 + s0

    def n(self, ahead):
        return self.s + ahead

    def last(self):
        return Step(self.s0 - 1, self.turn, self.full)

    def bank(self, use):
        k = USES_BEFORE[self.s0] + bank_uses(self.L).index(use)
        before = k // 2
        if self.turn is not None:
            per = (USES_BEFORE[self.s0 + 2] - USES_BEFORE[self.s0]) // 2
            before = self.turn * per + before
        return k % 2, before


def key_halves(st):
    return (1,) if st.L["B2"] == 1 and not st.full else (0, 1)


def after(eng, sem, count):
    if isinstance(count, int) and count <= 0:
        return
    eng.wait_ge(sem, count)


def run_steps(eng, step, short=None):
    for s in range(FIRST, 3):
        step(Step(s))
    with eng.Fori(0, 5) as turn:
        step(Step(3, turn))
        step(Step(4, turn))
    for s in range(13, BRANCH):
        step(Step(s))

    def layer_1(full):
        for s in range(BRANCH, 19):
            step(Step(s, full=full))
        with eng.Fori(0, 5) as turn:
            step(Step(19, turn, full))
            step(Step(20, turn, full))
        for s in range(29, LAST + 1):
            step(Step(s, full=full))

    if short is None:
        layer_1(True)
    else:
        with eng.If(short() == 1):
            layer_1(False)
        with eng.Else():
            layer_1(True)


def build(nc, xT, w0, w_ffn, w_out, w1, condT, cond_w, cond_b, rms_scale, mask, maskT, yT):
    ctx = ExitStack()
    with ctx:
        def sb(name, shape, dt):
            return ctx.enter_context(nc.sbuf_tensor(name, shape, dt))

        def pb(name):
            return ctx.enter_context(nc.psum_tensor(name, [P, 512], F32))

        def sem(name):
            return ctx.enter_context(nc.semaphore(name))

        X = sb("X", [P, B, FC, T], F32)
        Wh = sb("Wh", [P, 4, FC, D], F32R)
        Wl = sb("Wl", [P, 4, FC, D], F32R)
        Gh = sb("Gh", [P, 2, FC, HID], F32R)
        Gl = sb("Gl", [P, 2, FC, HID], F32R)
        Uh = sb("Uh", [P, HC, D], F32R)
        Ul = sb("Ul", [P, HC, D], F32R)
        stack = [sb(f"stack{i}", [P, 2, H, T], BF16) for i in range(2)]
        qst = [t[:, 0, :, :] for t in stack]
        kst = [t[:, 1, :, :] for t in stack]
        vaug = [sb(f"vaug{i}", [P, TC, H, VW], F32) for i in range(2)]
        E = sb("E", [P, E_RING, 2 * T], F32)
        nrm = sb("nrm", [P, FC, T], F32)
        xnh = [sb(f"xnh{i}", [P, FC, T], F32R) for i in range(2)]
        xnl = [sb(f"xnl{i}", [P, FC, T], F32R) for i in range(2)]
        dg = sb("dg", [P, 4, P], F32)
        crm = sb("crm", [P, FC, T], F32)
        xch = [sb(f"xch{i}", [P, FC, T], F32R) for i in range(2)]
        xcl = [sb(f"xcl{i}", [P, FC, T], F32R) for i in range(2)]
        rest = sb("rest", [P, FC, T], F32)
        qp = sb("qp", [P, 3, FC, T], BF16)
        kp = sb("kp", [P, 3, FC, T], BF16)
        oT = sb("oT", [P, 4, T], F32)
        on = sb("on", [P, TC, H, DH], F32)
        oh = sb("oh", [P, FC, T], F32R)
        ol = sb("ol", [P, FC, T], F32R)
        y = sb("y", [P, FC, T], F32)
        th = sb("th", [P, 2, T], F32)
        hf = sb("hf", [P, 2, T], F32)
        hh = sb("hh", [P, 2, T], F32R)
        hl = sb("hl", [P, 2, T], F32R)
        msk = sb("msk", [P, TC, T], BF16)
        mskT = sb("mskT", [P, TC, T], BF16)
        ident = sb("ident", [P, P], F32)
        identb = sb("identb", [P, P], BF16)
        ones = sb("ones", [P, P], F32)
        mean1 = sb("mean1", [P, 1], F32)
        cond = sb("cond", [P, CCH, B], F32)
        var = sb("var", [P, 4], F32)
        half_var = sb("half_var", [P, 4], F32)
        three_halves = sb("three_halves", [P, 4], F32)
        half = sb("half", [P, 4], F32)
        rstd = sb("rstd", [P, 4], F32)
        tmp4 = sb("tmp4", [P, 4], F32)
        nmax = sb("nmax", [P, 2, TC, 8], F32)
        nrest = sb("nrest", [P, TC, 8], F32)
        nparts = sb("nparts", [P, TC, 3, 8], BF16)
        nT = sb("nT", [24, T], BF16)
        rsum = sb("rsum", [P, TC, H], F32)
        cT = sb("cT", [DT, 2, B], F32)
        cth = sb("cth", [DT, B], F32)
        cb = sb("cb", [P, CCH], F32)
        rs = sb("rs", [P, FC], F32)
        hidden = sb("hidden", [P, 1], F32)
        short_flag = sb("short_flag", [P, 1], I32)

        s1ps = [pb(f"s1ps{i}") for i in range(2)]
        s2ps = [pb(f"s2ps{i}") for i in range(2)]
        pvps = pb("pvps")
        work = [pb(f"work{i}") for i in range(2)]
        acc = pb("acc")

        scr = [nc.dram_tensor(f"scr{i}", (2, 6 * DH, 8 * T), BF16, kind="Internal").ap() for i in range(2)]
        m_scr = [nc.dram_tensor(f"m_scr{i}", (24, T), BF16, kind="Internal").ap() for i in range(2)]

        x_loaded = sem("x_loaded")
        raw_loaded = [sem(f"raw_loaded{i}") for i in range(2)]
        small_loaded = sem("small_loaded")
        raw_hi = sem("raw_hi")
        raw_lo = sem("raw_lo")
        swap_loaded = sem("swap_loaded")
        swap_hi = sem("swap_hi")
        swap_lo = sem("swap_lo")
        consts = sem("consts")
        stack_ones = sem("stack_ones")
        setup = sem("setup")
        cond_tanh = sem("cond_tanh")
        cond_silu = sem("cond_silu")
        cond_mm = sem("cond_mm")
        cond_ready = sem("cond_ready")
        masks_ready = sem("masks_ready")
        hidden_ready, hidden_mm, flag_ready = sem("hidden_ready"), sem("hidden_mm"), sem("flag_ready")
        sq_n = sem("sq_n")
        sq_c = sem("sq_c")
        z_ready = sem("z_ready")
        work_full = [sem(f"work_full{i}") for i in range(2)]
        work_free = [sem(f"work_free{i}") for i in range(2)]
        newton = sem("newton")
        guess_order, guess_ready = sem("guess_order"), sem("guess_ready")
        diag_ready = sem("diag_ready")
        n_affine = sem("n_affine")
        n_hi = sem("n_hi")
        n_lo = sem("n_lo")
        c_affine = sem("c_affine")
        c_hi = sem("c_hi")
        c_lo = sem("c_lo")
        q_high, q_mid, q_low = sem("q_high"), sem("q_mid"), sem("q_low")
        k_high, k_mid, k_low = sem("k_high"), sem("k_mid"), sem("k_low")
        q_written, k_written = sem("q_written"), sem("k_written")
        stack_loaded = [sem(f"stack_loaded{i}") for i in range(2)]
        s1_full, s1_free = sem("s1_full"), sem("s1_free")
        shift_order, shift_parts = sem("shift_order"), sem("shift_parts")
        shift_written = sem("shift_written")
        shift_loaded = [sem(f"shift_loaded{i}") for i in range(2)]
        s2_full, exp_done = sem("s2_full"), sem("exp_done")
        pv_done, oT_ready = sem("pv_done"), sem("oT_ready")
        sums_inv = sem("sums_inv")
        o_high = sem("o_high")
        tanh_ready, silu_ready = sem("tanh_ready"), sem("silu_ready")
        h_high, h_low = sem("h_high"), sem("h_low")
        down_done, x1_ready = sem("down_done"), sem("x1_ready")
        out_ready, out_stored = sem("out_ready"), sem("out_stored")

        raw = [E[:, 4 * i:4 * i + 4, :] for i in range(2)]
        RAW = [
            (w0.rearrange("w (c p) n -> p (w c) n", p=P), Wh[:, :, :, :].rearrange("p w c n -> p (w c n)"),
             Wl[:, :, :, :].rearrange("p w c n -> p (w c n)")),
        ] + [
            (w_ffn[i].rearrange("(c p) n -> p c n", p=P), Gh[:, i, :, :].rearrange("p c n -> p (c n)"),
             Gl[:, i, :, :].rearrange("p c n -> p (c n)")) for i in range(2)
        ] + [
            (w_out.rearrange("(c p) n -> p c n", p=P), Uh[:, :, :].rearrange("p c n -> p (c n)"),
             Ul[:, :, :].rearrange("p c n -> p (c n)")),
        ]
        SWAPS = {13: [0, 1], 14: [2], 16: [3]}

        def flat(ap):
            return ap.rearrange("p a b -> p (a b)")

        block = ctx.enter_context(nc.Block())

        @block.sync
        def _(sp):
            def load_x(n):
                sp.dma_start(X[:, bass.ds(n, 1), :, :].rearrange("p o c t -> p (o c) t"),
                             xT[:, :, bass.ds(n * T, T)].rearrange("c p t -> p c t")).then_inc(x_loaded, 16)

            load_x(0)
            for i, (src, _, _) in enumerate(RAW):
                if i >= 2:
                    after(sp, raw_lo, i - 1)
                sp.dma_start(raw[i % 2].rearrange("p a b -> p (a b)").rearrange(
                    "p (c n) -> p c n", c=src.shape[1]), src).then_inc(raw_loaded[i % 2], 16)
                if i == 1:
                    for dst, s in ((cT[:, 0, :], condT), (cb[:, :], cond_b), (rs[:, :], rms_scale)):
                        sp.dma_start(dst, s).then_inc(small_loaded, 16)
                    sp.dma_start(y[0:DT, :, :].rearrange("p a b -> p (a b)"), cond_w[:, 0:512]).then_inc(small_loaded, 16)
                    sp.dma_start(rest[0:DT, :, :].rearrange("p a b -> p (a b)"), cond_w[:, 512:1024]).then_inc(small_loaded, 16)
                    sp.dma_start(crm[0:DT, :, :].rearrange("p a b -> p (a b)"), cond_w[:, 1024:1536]).then_inc(small_loaded, 16)
                    sp.dma_start(hf[:, 0, 0:P].bitcast(I32).rearrange("p (c t) -> p c t", c=TC), mask).then_inc(small_loaded, 16)
                    sp.dma_start(hf[:, 1, 0:P].bitcast(I32).rearrange("p (c t) -> p c t", c=TC), maskT).then_inc(small_loaded, 16)

            def write_parts(par, row, parts, written):
                for part in range(3):
                    for c in range(FC):
                        dst = scr[par][c, row + DH * part:row + DH * (part + 1), :]
                        sp.dma_start(dst.rearrange("d (h t) -> h d t", h=8),
                                     parts[:, part, c, :]).then_inc(written, 16)

            def read_stack(par, half_):
                row = 0
                for parts in (3, 2, 1):
                    k = DH * parts
                    src = bass.AP(scr[par].tensor, half_ * 6 * DH * 8 * T,
                                  [[8 * T, k], [(6 * DH - k) * 8 * T, 2], [1, 8 * T]])
                    dst = stack[par][row:row + k, :, 8 * half_:8 * half_ + 8, :]
                    sp.dma_start(dst.rearrange("r o h t -> r o (h t)"), src).then_inc(stack_loaded[half_], 16)
                    row += k

            def step(st):
                L, par = st.L, st.par

                registers = []

                def held(count):
                    if isinstance(count, int):
                        return count
                    registers.append(nc.sync.alloc_register(f"held{st.s0}_{len(registers)}"))
                    nc.sync.reg_mov(registers[-1], count)
                    return nc.sync.snap(registers[-1], min_val=0, max_val=1 << 20)

                n_x, n_a, n_b1, n_b2 = st.n(3), st.n(2), st.n(1), st.n(0)
                x_before = held(16 * n_x)
                scratch_read = held(48 * (n_a - 1))
                a_split = held(n_a + 1)
                a_written = held(96 * (n_a + 1))
                heads_used = [held(UNITS * n_b2 + 8), held(UNITS * n_b2 + 16)]
                rows_used = held(UNITS * n_b2)
                rows_read = held(16 * n_b1)
                rows_written = [held(16 * (2 * n_b1 + 1)), held(16 * (2 * n_b1 + 2))]
                rows_made = [None, None]
                if L["B1"] is not None:
                    for half_ in range(2):
                        b, k = st.bank(f"sh{half_}")
                        rows_made[half_] = (work_free[b], held(k + 1))
                result_made = held(st.n(-1 - B) + 1)

                def shift_rows(half_):
                    after(sp, shift_loaded[half_], rows_read)
                    after(sp, *rows_made[half_])
                    sp.dma_start(m_scr[half_], nT[:, :]).then_inc(shift_written, 16)
                    if L["B2"] is not None:
                        after(sp, s2_full, rows_used)
                    after(sp, shift_written, rows_written[half_])
                    sp.dma_start(qst[1 - par][PARTS:ROWS, 8 * half_:8 * half_ + 8, :],
                                 m_scr[half_].rearrange("(r h) t -> r h t", r=3)).then_inc(shift_loaded[half_], 16)

                if L["N"] == 0 and st.s0 > FIRST:
                    after(sp, x_loaded, x_before)
                    load_x(n_x)
                if L["A"] is not None:
                    for half_ in range(2):
                        after(sp, stack_loaded[half_], scratch_read)
                    after(sp, q_low, a_split)
                    write_parts(par, 0, qp, q_written)
                    after(sp, k_low, a_split)
                    write_parts(par, 3 * DH, kp, k_written)
                if L["B1"] is not None:
                    shift_rows(0)
                if L["A"] is not None:
                    after(sp, q_written, a_written)
                    after(sp, k_written, a_written)
                    if L["B2"] is not None:
                        after(sp, s2_full, heads_used[0])
                    read_stack(par, 0)
                if L["B1"] is not None:
                    shift_rows(1)
                if L["A"] is not None:
                    if L["B2"] is not None:
                        after(sp, s2_full, heads_used[1])
                    read_stack(par, 1)
                for m in SWAPS.get(st.s0, ()):
                    after(sp, swap_lo, m)
                    if m == 0:
                        sp.wait_ge(n_lo, B)
                        sp.wait_ge(n_hi, B)
                    sp.dma_start(nrm[:, :, :], w1[m].rearrange("(c p) n -> p c n", p=P)).then_inc(swap_loaded, 16)
                if L["C"] == 1:
                    n = st.n(-1 - B)
                    after(sp, out_ready, result_made)
                    sp.dma_start(yT[:, :, bass.ds(n * T, T)].rearrange("c p t -> p c t"), crm[:, :, :])\
                      .then_inc(out_stored, 16)
                for r in registers:
                    nc.sync.free_register(r)

            run_steps(nc.sync, step)
            sp.wait_ge(out_stored, 16 * B)

        @block.tensor
        def _(pe):
            mm = nc.tensor.matmul

            def mm3(out, lh, ll, rh, rl, first, last):
                mm(out, lh, rh, start=first, stop=False, skip_group_check=True)
                mm(out, lh, rl, start=False, stop=False, skip_group_check=True)
                return mm(out, ll, rh, start=False, stop=last, skip_group_check=True)

            pe.wait_ge(small_loaded, 16 * 8)
            pe.wait_ge(cond_silu, 1)
            for c in range(CCH):
                src = (y, rest, crm)[c // 4][0:DT, :, :].rearrange("p a b -> p (a b)")
                last = mm(acc[:, B * c:B * (c + 1)], src[:, P * (c % 4):P * (c % 4 + 1)],
                          cT[:, 0 if c < 8 else 1, :], start=True, stop=True)
            last.then_inc(cond_mm, 1)
            pe.wait_ge(consts, 5)
            pe.wait_ge(stack_ones, 2)
            pe.wait_ge(hidden_ready, 1)
            pe.wait_ge(cond_ready, 2)
            mm(acc[:, 0:1], ones[:, :], hidden[:, :], start=True, stop=True).then_inc(hidden_mm, 1)

            def open_bank(st, use):
                b, k = st.bank(use)
                after(pe, work_free[b], k)
                return work[b], work_full[b]

            def project_T(out, w, xh, xl, chunks=FC):
                for m in range(FC):
                    for c in range(chunks):
                        last = mm3(out[:, m * T:(m + 1) * T], Wh[:, w, c, P * m:P * (m + 1)],
                                   Wl[:, w, c, P * m:P * (m + 1)], xh[:, c, :], xl[:, c, :],
                                   c == 0, c == chunks - 1)
                return last

            def scores_for_max(st, g):
                n, par = st.n(1), 1 - st.par
                if g in (0, 4):
                    after(pe, stack_loaded[g // 4], 48 * (n + 1))
                if not st.full:
                    after(pe, s1_free, UNITS * n + 2 * g - 2)
                    bank = s1ps[g % 2]
                    for qh in range(TC):
                        out = bank[:, T * qh:T * (qh + 1)]
                        mm(out.rearrange("p (h t) -> p h t", h=2), identb[:, :],
                           msk[:, qh, P:T][:, None, :].to_broadcast([P, 2, P]),
                           start=True, stop=False, skip_group_check=True)
                        for i in range(2):
                            h = 2 * g + i
                            last = mm(out[:, P * i:P * (i + 1)], qst[par][0:PARTS, h, P * qh:P * (qh + 1)],
                                      kst[par][0:PARTS, h, P:T], start=False, stop=True,
                                      skip_group_check=True)
                    last.then_inc(s1_full, 2)
                    return
                for qh in range(TC):
                    u = 2 * g + qh
                    after(pe, s1_free, UNITS * n + u - 1)
                    bank = s1ps[u % 2]
                    if st.L["B1"] == 1:
                        mm(bank[:, :].rearrange("p (h t) -> p h t", h=2), identb[:, :],
                           msk[:, qh, :][:, None, :].to_broadcast([P, 2, T]),
                           start=True, stop=False, skip_group_check=True)
                    for i in range(2):
                        h = 2 * g + i
                        last = mm(bank[:, T * i:T * (i + 1)], qst[par][0:PARTS, h, P * qh:P * (qh + 1)],
                                  kst[par][0:PARTS, h, :], start=st.L["B1"] == 0, stop=True,
                                  skip_group_check=True)
                    last.then_inc(s1_full, 1)

            def scores(st, g):
                n, par = st.n(0), st.par
                if g in (0, 4):
                    after(pe, shift_loaded[g // 4], 16 * (n + 1))
                short = st.L["B2"] == 1 and not st.full
                for kh in key_halves(st):
                    u = 2 * g + kh
                    after(pe, exp_done, UNITS * n + (2 * g - 2 if short else u - 1))
                    bank = s2ps[g % 2 if short else u % 2]
                    if st.L["B2"] == 1:
                        mm(bank[:, :].rearrange("p (h t) -> p h t", h=2), identb[:, :],
                           mskT[:, kh, :][:, None, :].to_broadcast([P, 2, T]),
                           start=True, stop=False, skip_group_check=True)
                    for i in range(2):
                        h = 2 * g + i
                        last = mm(bank[:, T * i:T * (i + 1)], kst[par][0:ROWS, h, P * kh:P * (kh + 1)],
                                  qst[par][0:ROWS, h, :], start=st.L["B2"] == 0, stop=True,
                                  skip_group_check=True)
                    last.then_inc(s2_full, 2 if short else 1)

            def values(st, j):
                n = st.n(0)
                after(pe, exp_done, UNITS * n + 4 * j + 4)
                if j % 2 == 0:
                    after(pe, oT_ready, 2 * n + j // 2)
                for kh in key_halves(st):
                    for i in range(4):
                        h = 4 * j + i
                        u = 2 * (h // 2) + kh
                        last = mm(pvps[32 * i:32 * (i + 1), T * (j % 2):T * (j % 2 + 1)],
                                  vaug[st.par][:, kh, h, :], E[:, u % E_RING, T * (h % 2):T * (h % 2 + 1)],
                                  start=kh == key_halves(st)[0], stop=kh == TC - 1, skip_group_check=True)
                last.then_inc(pv_done, 1)

            def swiglu_up(st, i):
                bank, full = open_bank(st, f"F{i}")
                if i == 0:
                    after(pe, c_lo, st.n(-2) + 1)
                for w in range(2):
                    for c in range(FC):
                        last = mm3(bank[:, T * w:T * (w + 1)], Gh[:, w, c, P * i:P * (i + 1)],
                                   Gl[:, w, c, P * i:P * (i + 1)], xch[st.par][:, c, :],
                                   xcl[st.par][:, c, :], c == 0, c == FC - 1)
                last.then_inc(full, 1)

            def swiglu_down(n, i):
                after(pe, h_low, HC * n + i + 1)
                if i == 0:
                    after(pe, x1_ready, n)
                for m in range(FC):
                    last = mm3(acc[:, T * m:T * (m + 1)], Uh[:, i, P * m:P * (m + 1)],
                               Ul[:, i, P * m:P * (m + 1)], hh[:, i % 2, :], hl[:, i % 2, :],
                               i == 0 and m == 0, i == HC - 1)
                last.then_inc(down_done, 1)

            def divide_in(st):
                after(pe, oT_ready, 2 * st.n(-1) + 2)
                for qh, use in enumerate(("T1a", "T1b")):
                    bank, full = open_bank(st, use)
                    for j in range(4):
                        last = nc.tensor.transpose(bank[:, P * j:P * (j + 1)], oT[:, j, P * qh:P * (qh + 1)],
                                                   ident[:, :])
                    last.then_inc(full, 1)

            def divide_out(st):
                for use in ("T1a", "T1b"):
                    b, k = st.bank(use)
                    after(pe, work_free[b], k + 1)
                bank, full = open_bank(st, "T2")
                for m in range(FC):
                    for qh in range(TC):
                        src = on[:, qh, 8 * m:8 * m + 8, :].rearrange("p h d -> p (h d)")
                        last = nc.tensor.transpose(bank[:, T * m + P * qh:T * m + P * (qh + 1)], src,
                                                   ident[:, :])
                last.then_inc(full, 1)

            def value_projection(st):
                n = st.n(1)
                par = 1 - st.par
                after(pe, n_lo, n + 1)
                bank, full = open_bank(st, "V")
                for t in range(TC):
                    for c in range(FC):
                        last = mm3(bank[:, D * t:D * (t + 1)], xnh[par][:, c, P * t:P * (t + 1)],
                                   xnl[par][:, c, P * t:P * (t + 1)], Wh[:, 2, c, :], Wl[:, 2, c, :],
                                   c == 0, c == FC - 1)
                last.then_inc(full, 1)

            def output_projection(st):
                b, k = st.bank("T2")
                after(pe, work_free[b], k + 1)
                bank, full = open_bank(st, "Wo")
                project_T(bank, 3, oh, ol).then_inc(full, 1)

            def qk_projection(st, use, w):
                after(pe, n_lo, st.n(2) + 1)
                bank, full = open_bank(st, use)
                project_T(bank, w, xnh[st.par], xnl[st.par]).then_inc(full, 1)

            def mean_squares(st):
                bank, full = open_bank(st, "ms")
                jobs = []
                if st.L["N"] == 0:
                    after(pe, sq_n, st.n(3) + 1)
                    jobs.append((nrm[:, :, :], 0))
                if st.L["C"] is not None:
                    after(pe, sq_c, st.n(-1) + 1)
                    jobs.append((dg[:, :, :].rearrange("p (c u) t -> p c (u t)", c=FC), 2))
                for src, col in jobs:
                    for t in range(TC):
                        for c in range(FC):
                            last = mm(bank[:, col + t:col + t + 1], src[:, c, P * t:P * (t + 1)],
                                      mean1[:, :], start=c == 0, stop=c == FC - 1, skip_group_check=True)
                last.then_inc(full, 1)

            def broadcast_rstd(st, use, col):
                bank, full = open_bank(st, use)
                after(pe, diag_ready, st.n(3) + 1)
                mm(bank[:, 0:T], ones[:, :], dg[:, col:col + 2, :].rearrange("p a b -> p (a b)"),
                   start=True, stop=True).then_inc(full, 1)

            def shift_transpose(st, half_):
                bank, full = open_bank(st, f"sh{half_}")
                after(pe, shift_parts, 2 * st.n(1) + half_ + 1)
                out = bank[0:24, 0:P].bitcast(BF16)
                for qh in range(TC):
                    last = nc.tensor.transpose(out[:, P * qh:P * (qh + 1)],
                                               nparts[:, qh, :, :].rearrange("p r h -> p (r h)"), identb[:, :])
                last.then_inc(full, 1)

            def step(st):
                L = st.L
                if st.s0 == FIRST:
                    pe.wait_ge(raw_lo, 4)
                if st.s0 == B - 1:
                    pe.wait_ge(masks_ready, 2)
                for g in range(SLOTS):
                    if L["B1"] is not None:
                        scores_for_max(st, g)
                    if L["B2"] is not None:
                        scores(st, g)
                        if g in (2, 4, 6):
                            values(st, g // 2 - 1)
                    if g == 0 and L["C"] is not None:
                        divide_in(st)
                    if g == 1:
                        if L["C"] is not None:
                            divide_out(st)
                        if L["V"] is not None:
                            if st.s0 + 1 == B:
                                pe.wait_ge(swap_lo, 3)
                            value_projection(st)
                    if g == 2:
                        if L["C"] is not None:
                            if st.s0 - 1 == B:
                                pe.wait_ge(swap_lo, 4)
                            output_projection(st)
                        if L["A"] is not None:
                            if st.s0 + 2 == B:
                                pe.wait_ge(swap_lo, 2)
                            qk_projection(st, "Q", 0)
                    if g == 3 and L["A"] is not None:
                        qk_projection(st, "K", 1)
                    if g == 4:
                        if L["N"] == 0 or L["C"] is not None:
                            mean_squares(st)
                        if L["B1"] is not None:
                            shift_transpose(st, 0)
                    if g == 6:
                        if L["C"] is not None:
                            broadcast_rstd(st, "bcC", 2)
                        if L["N"] == 0:
                            broadcast_rstd(st, "bcN", 0)
                    if L["C2"] is not None:
                        swiglu_up(st, g)
                        if g >= 2:
                            swiglu_down(st.n(-2), g - 2)
                    if g < 2 and L["C3"] is not None:
                        swiglu_down(st.n(-3), HC - 2 + g)
                if L["B2"] is not None:
                    values(st, 3)
                if L["B1"] is not None:
                    shift_transpose(st, 1)

            def short():
                pe.wait_ge(flag_ready, 1)
                return nc.tensor.value_load(short_flag[0:1, 0:1], min_val=0, max_val=1)

            run_steps(nc.tensor, step, short)

        @block.vector
        def _(dve):
            v = nc.vector
            for i in range(2):
                v.memset(kst[i][PARTS:ROWS, :, :], 1.0).then_inc(stack_ones, 1)
            for i, (_, hi, lo) in enumerate(RAW):
                dve.wait_ge(raw_loaded[i % 2], 16 * (i // 2 + 1))
                dve.wait_ge(raw_hi, i + 1)
                v.tensor_tensor(lo, flat(raw[i % 2]), hi.bitcast(F32), ALU.subtract).then_inc(raw_lo, 1)
                if i == 0:
                    dve.wait_ge(cond_tanh, 1)
                    v.tensor_scalar(cth[:, :], cth[:, :], 0.5, 0.5, ALU.mult, ALU.add).then_inc(setup, 1)
                    dve.wait_ge(setup, 1)
                    v.tensor_tensor(cT[:, 1, :], cth[:, :], cT[:, 0, :], ALU.mult).then_inc(cond_silu, 1)
                    v.tensor_scalar(msk[:, :, :], hf[:, 0, 0:P].bitcast(U8).rearrange("p (c t) -> p c t", c=TC),
                                    NEG, None, ALU.mult).then_inc(masks_ready, 1)
                    v.tensor_scalar(mskT[:, :, :], hf[:, 1, 0:P].bitcast(U8).rearrange("p (c t) -> p c t", c=TC),
                                    NEG, None, ALU.mult).then_inc(masks_ready, 1)
                    v.tensor_reduce(hidden[:, :], hf[:, 0, 0:P].bitcast(U8)
                                    .rearrange("p (c t) -> p c t", c=TC)[:, :, 0:P],
                                    mybir.AxisListType.XY, ALU.add).then_inc(hidden_ready, 1)
                    dve.wait_ge(cond_mm, 1)
                    v.tensor_tensor(cond[:, :, :], acc[:, 0:CCH * B].rearrange("p (c b) -> p c b", c=CCH),
                                    cb[:, :][:, :, None].to_broadcast([P, CCH, B]), ALU.add).then_inc(setup, 1)
                    dve.wait_ge(setup, 2)
                    for c in range(FC):
                        v.tensor_scalar(cond[:, C_SCALE + c, :], cond[:, C_SCALE + c, :], 1.0,
                                        rs[:, c:c + 1], ALU.add, ALU.mult).then_inc(cond_ready, 1)
            dve.wait_ge(consts, 5)
            dve.wait_ge(hidden_mm, 1)
            v.tensor_scalar(short_flag[:, :], acc[:, 0:1], T * P - 0.5, None, ALU.is_ge)\
             .then_inc(flag_ready, 1)

            def maxima(st, g):
                n = st.n(1)
                if not st.full:
                    after(dve, s1_full, UNITS * n + 2 * g + 2)
                    v.tensor_reduce(nmax[:, g // 4, :, 2 * (g % 4):2 * (g % 4) + 2],
                                    s1ps[g % 2][:, :].rearrange("p (q h t) -> p q h t", q=2, h=2), AX_X,
                                    ALU.max, negate=True).then_inc(s1_free, 2)
                    return
                for qh in range(TC):
                    u = 2 * g + qh
                    after(dve, s1_full, UNITS * n + u + 1)
                    v.tensor_reduce(nmax[:, g // 4, qh, 2 * (g % 4):2 * (g % 4) + 2],
                                    s1ps[u % 2][:, :].rearrange("p (h t) -> p h t", h=2), AX_X, ALU.max,
                                    negate=True).then_inc(s1_free, 1)

            def shift_split(st, half_):
                n = st.n(1)
                k = 2 * n + half_
                done = SHIFT_OPS * k
                nm = nmax[:, half_, :, :]
                after(dve, s1_free, UNITS * n + 8 * half_ + 8)
                v.tensor_scalar(nm, nm, CLAMP, None, ALU.min).then_inc(shift_order, 1)
                after(dve, shift_order, done + 1)
                if half_ or st.s0 >= 0:
                    b, k = st.bank("sh0") if half_ else st.last().bank("sh1")
                    after(dve, work_full[b], k + 1)
                v.tensor_copy(nparts[:, :, 0, :], nm).then_inc(shift_order, 1)
                after(dve, shift_order, done + 2)
                v.tensor_tensor(nrest[:, :, :], nm, nparts[:, :, 0, :], ALU.subtract).then_inc(shift_order, 1)
                after(dve, shift_order, done + 3)
                v.tensor_copy(nparts[:, :, 1, :], nrest[:, :, :]).then_inc(shift_order, 1)
                after(dve, shift_order, done + 4)
                v.tensor_tensor(nparts[:, :, 2, :], nrest[:, :, :], nparts[:, :, 1, :],
                                ALU.subtract).then_inc(shift_parts, 1)

            def opened(st, use):
                b, k = st.bank(use)
                after(dve, work_full[b], k + 1)
                return work[b], work_free[b]

            def divide(st):
                for qh, use in enumerate(("T1a", "T1b")):
                    bank, free = opened(st, use)
                    heads = bank[:, :].rearrange("p (h w) -> p h w", w=VW)
                    v.reciprocal(rsum[:, qh, :], heads[:, :, DH]).then_inc(sums_inv, 1)
                    after(dve, sums_inv, TC * st.n(-1) + qh + 1)
                    v.tensor_tensor(on[:, qh, :, :], heads[:, :, 0:DH],
                                    rsum[:, qh, :][:, :, None].to_broadcast([P, H, DH]), ALU.mult)\
                     .then_inc(free, 1)

            def o_split(st):
                bank, free = opened(st, "T2")
                after(dve, o_high, st.n(-1) + 1)
                v.tensor_tensor(flat(ol[:, :, :]), bank[:, :], flat(oh[:, :, :]).bitcast(F32), ALU.subtract)\
                 .then_inc(free, 1)

            def qk_split(st, use, parts, hi_at, high, mid, low):
                n = st.n(2)
                bank, free = opened(st, use)
                after(dve, high, n + 1)
                after(dve, k_low if use == "Q" else q_low, n if use == "Q" else n + 1)
                v.tensor_tensor(flat(rest[:, :, :]), bank[:, :],
                                parts[:, hi_at, :, :].rearrange("p c t -> p (c t)"), ALU.subtract).then_inc(free, 1)
                b, k = st.bank(use)
                after(dve, work_free[b], k + 1)
                v.tensor_copy(parts[:, 1, :, :], rest[:, :, :]).then_inc(mid, 1)

            def attention_residual(st):
                n = st.n(-1)
                bank, free = opened(st, "Wo")
                after(dve, z_ready, n)
                v.tensor_tensor(flat(y[:, :, :]), bank[:, :],
                                X[:, bass.ds(n, 1), :, :].rearrange("p o c t -> p (o c t)"), ALU.add)\
                 .then_inc(free, 1)

            def rsqrt(st):
                lo = 0 if st.L["N"] == 0 else 2
                hi = 4 if st.L["C"] is not None else 2
                c = slice(lo, hi)
                bank, free = opened(st, "ms")
                v.tensor_scalar(half_var[:, c], bank[:, c], EPS, -0.5, ALU.add, ALU.mult).then_inc(guess_order, 1)
                v.tensor_scalar(var[:, c], bank[:, c], EPS, None, ALU.add).then_inc(free, 1)
                b, k = st.bank("ms")
                after(dve, work_free[b], k + 1)
                v.tensor_scalar(half[:, c].bitcast(I32), var[:, c].bitcast(I32), 1, None,
                                ALU.logical_shift_right).then_inc(guess_order, 1)
                after(dve, guess_order, 2 * st.n(3) + 2)
                v.tensor_scalar(rstd[:, c].bitcast(I32), half[:, c].bitcast(I32), -1.0, RSQRT_MAGIC,
                                ALU.mult, ALU.add).then_inc(guess_ready, 1)

            def diagonals(st):
                lo = 0 if st.L["N"] == 0 else 2
                hi = 4 if st.L["C"] is not None else 2
                c = slice(lo, hi)
                after(dve, newton, NEWTON_OPS * (st.n(3) + 1))
                v.tensor_tensor(dg[:, c, :], ident[:, :][:, None, :].to_broadcast([P, hi - lo, P]),
                                rstd[:, c][:, :, None].to_broadcast([P, hi - lo, P]), ALU.mult)\
                 .then_inc(diag_ready, 1)

            def normalize(st, use, dst, src):
                bank, free = opened(st, use)
                v.tensor_tensor(dst, src, bank[:, 0:T][:, None, :].to_broadcast([P, FC, T]), ALU.mult)\
                 .then_inc(free, 1)

            def swiglu(st, i):
                n = st.n(-2)
                bank, free = opened(st, f"F{i}")
                after(dve, tanh_ready, HC * n + i + 1)
                v.scalar_tensor_tensor(th[:, i % 2, :], th[:, i % 2, :], 1.0, bank[:, 0:T],
                                       ALU.add, ALU.mult).then_inc(silu_ready, 1)
                after(dve, silu_ready, HC * n + i + 1)
                after(dve, h_low, HC * n + i - 1)
                v.scalar_tensor_tensor(hf[:, i % 2, :], th[:, i % 2, :], 0.5, bank[:, T:2 * T],
                                       ALU.mult, ALU.mult).then_inc(free, 1)

            def step(st):
                L = st.L
                for g in range(SLOTS):
                    if L["B1"] is not None:
                        maxima(st, g)
                    if g == 0 and L["C"] is not None:
                        divide(st)
                    if g == 1 and L["C"] is not None:
                        o_split(st)
                    if g == 2:
                        if L["C"] == 0:
                            attention_residual(st)
                        if L["A"] is not None:
                            qk_split(st, "Q", qp, 0, q_high, q_mid, q_low)
                        if L["C3"] is not None:
                            n = st.n(-3)
                            after(dve, down_done, HC * (n + 1))
                            x_n = X[:, bass.ds(n, 1), :, :].rearrange("p o c t -> p (o c t)")
                            v.tensor_tensor(x_n, acc[:, :], x_n, ALU.add).then_inc(x1_ready, 1)
                    if g == 3:
                        if L["A"] is not None:
                            qk_split(st, "K", kp, 2, k_high, k_mid, k_low)
                    if g == 4:
                        if L["B1"] is not None:
                            shift_split(st, 0)
                        if L["N"] == 0 or L["C"] is not None:
                            rsqrt(st)
                    if g == 6 and (L["N"] == 0 or L["C"] is not None):
                        diagonals(st)
                        if L["C"] is not None:
                            if L["C"] == 1:
                                after(dve, out_stored, 16 * (st.n(-1) - B))
                            normalize(st, "bcC", crm[:, :, :], y[:, :, :])
                        if L["N"] == 0:
                            n = st.n(3)
                            normalize(st, "bcN", nrm[:, :, :],
                                      X[:, bass.ds(n, 1), :, :].rearrange("p o c t -> p (o c) t"))
                    if L["C2"] is not None:
                        swiglu(st, g)
                if L["B1"] is not None:
                    shift_split(st, 1)
                for m in SWAPS.get(st.s0, ()):
                    dve.wait_ge(swap_hi, m + 1)
                    v.tensor_tensor(Wl[:, m, :, :], nrm[:, :, :], Wh[:, m, :, :].bitcast(F32),
                                    ALU.subtract).then_inc(swap_lo, 1)

            def short():
                dve.wait_ge(flag_ready, 1)
                return nc.vector.value_load(short_flag[0:1, 0:1], min_val=0, max_val=1)

            run_steps(nc.vector, step, short)

        @block.scalar
        def _(act):
            a = nc.scalar
            for i, (_, hi, lo) in enumerate(RAW):
                act.wait_ge(raw_loaded[i % 2], 16 * (i // 2 + 1))
                a.copy(hi, flat(raw[i % 2])).then_inc(raw_hi, 1)
                if i == 0:
                    act.wait_ge(small_loaded, 16 * 8)
                    a.activation(cth[:, :], cT[:, 0, :], ACT.Tanh, scale=0.5).then_inc(cond_tanh, 1)
            act.wait_ge(cond_ready, 2)

            def opened(st, use):
                b, k = st.bank(use)
                after(act, work_full[b], k + 1)
                return work[b], work_free[b]

            def exps(st, g):
                n = st.n(0)
                short = st.L["B2"] == 1 and not st.full
                for kh in key_halves(st):
                    u = 2 * g + kh
                    after(act, s2_full, UNITS * n + u + 1)
                    after(act, pv_done, 4 * n + u // 4 - 1)
                    a.activation(E[:, u % E_RING, :], s2ps[g % 2 if short else u % 2][:, :], ACT.Exp,
                                 scale=SCORE_SCALE).then_inc(exp_done, 2 if short else 1)

            def store_oT(st, pair):
                n = st.n(0)
                after(act, pv_done, 4 * n + 2 * pair + 2)
                if pair == 0 and st.L["C"] is not None:
                    for use in ("T1a", "T1b"):
                        b, k = st.bank(use)
                        after(act, work_full[b], k + 1)
                a.copy(oT[:, 2 * pair:2 * pair + 2, :], pvps[:, :].rearrange("p (j t) -> p j t", j=2))\
                 .then_inc(oT_ready, 1)

            def tanh(st, i):
                bank, _ = opened(st, f"F{i}")
                if i >= 2:
                    b, k = st.bank(f"F{i - 2}")
                    after(act, work_free[b], k + 1)
                a.activation(th[:, i % 2, :], bank[:, 0:T], ACT.Tanh, scale=0.5).then_inc(tanh_ready, 1)

            def h_high_part(st, n, i):
                b, k = st.bank(f"F{i}")
                after(act, work_free[b], k + 1)
                after(act, down_done, HC * n + i - 1)
                a.copy(hh[:, i % 2, :], hf[:, i % 2, :]).then_inc(h_high, 1)

            def affine(st, buf, gain, shift, b, done, count):
                for c in range(FC):
                    a.activation(buf[:, c, :], buf[:, c, :], ACT.Identity,
                                 scale=cond[:, gain + c, bass.ds(b, 1)],
                                 bias=cond[:, shift + c, bass.ds(b, 1)]).then_inc(done, 1)
                after(act, done, count)

            def step(st):
                L = st.L
                for g in range(SLOTS):
                    if L["B2"] is not None:
                        exps(st, g)
                    if g == 1:
                        if L["C"] is not None:
                            bank, _ = opened(st, "T2")
                            a.copy(flat(oh[:, :, :]), bank[:, :]).then_inc(o_high, 1)
                        if L["V"] is not None:
                            bank, free = opened(st, "V")
                            after(act, pv_done, 4 * st.n(0))
                            a.copy(vaug[1 - st.par][:, :, :, 0:DH],
                                   bank[:, :].rearrange("p (t h d) -> p t h d", t=TC, h=H)).then_inc(free, 1)
                    if g == 2:
                        if L["C"] == 1:
                            bank, free = opened(st, "Wo")
                            b, k = st.last().bank("bcC")
                            after(act, work_free[b], k + 1)
                            if st.s0 - 1 == B:
                                act.wait_ge(z_ready, B)
                            a.copy(flat(y[:, :, :]), bank[:, :]).then_inc(free, 1)
                        if L["A"] is not None:
                            bank, _ = opened(st, "Q")
                            after(act, q_written, 96 * st.n(2))
                            a.copy(qp[:, 0, :, :].rearrange("p c t -> p (c t)"), bank[:, :]).then_inc(q_high, 1)
                    if g == 3 and L["A"] is not None:
                        bank, _ = opened(st, "K")
                        after(act, k_written, 96 * st.n(2))
                        a.copy(kp[:, 2, :, :].rearrange("p c t -> p (c t)"), bank[:, :]).then_inc(k_high, 1)
                    if g == 4 and L["N"] == 1:
                        n = st.n(3)
                        after(act, x1_ready, n - B + 1)
                        a.copy(xnh[1 - st.par][:, :, :],
                               X[:, bass.ds(n - B, 1), :, :].rearrange("p o c t -> p (o c) t")).then_inc(n_hi, 1)
                    if g == 5:
                        if L["B2"] is not None:
                            store_oT(st, 0)
                        if L["B1"] is not None:
                            shift_store(st, 0)
                    if g == 7:
                        if L["C"] is not None:
                            n = st.n(-1)
                            b, k = st.bank("bcC")
                            after(act, work_free[b], k + 1)
                            if L["C"] == 0:
                                affine(st, crm, C_G2, C_B2, n, c_affine, 2 * (n + 1))
                                a.copy(xch[1 - st.par][:, :, :], crm[:, :, :]).then_inc(c_hi, 1)
                            else:
                                affine(st, crm, C_SCALE, C_SHIFT, n - B, c_affine, 2 * (n + 1))
                        if L["N"] == 0:
                            n = st.n(3)
                            b, k = st.bank("bcN")
                            after(act, work_free[b], k + 1)
                            affine(st, nrm, C_G1, C_B1, n, n_affine, 2 * (n + 1))
                            a.copy(xnh[1 - st.par][:, :, :], nrm[:, :, :]).then_inc(n_hi, 1)
                    if L["C2"] is not None:
                        tanh(st, g)
                        if g >= 1:
                            h_high_part(st, st.n(-2), g - 1)
                    if g == 0 and L["C3"] is not None:
                        h_high_part(st.last(), st.n(-3), HC - 1)
                if L["B2"] is not None:
                    store_oT(st, 1)
                if L["B1"] is not None:
                    shift_store(st, 1)
                for m in SWAPS.get(st.s0, ()):
                    act.wait_ge(swap_loaded, 16 * (m + 1))
                    if m == 0:
                        b, k = st.bank("K")
                        act.wait_ge(work_full[b], k + 1)
                    if m == 2:
                        b, k = st.bank("V")
                        act.wait_ge(work_full[b], k + 1)
                    if m == 3:
                        b, k = st.bank("Wo")
                        act.wait_ge(work_full[b], k + 1)
                    a.copy(Wh[:, m, :, :], nrm[:, :, :]).then_inc(swap_hi, 1)

            def shift_store(st, half_):
                bank, free = opened(st, f"sh{half_}")
                after(act, shift_written, 16 * (2 * st.n(1) + half_))
                a.copy(nT[:, :], bank[0:24, 0:P].bitcast(BF16)).then_inc(free, 1)

            def short():
                act.wait_ge(flag_ready, 1)
                return nc.scalar.value_load(short_flag[0:1, 0:1], min_val=0, max_val=1)

            run_steps(nc.scalar, step, short)

        @block.gpsimd
        def _(pool):
            p = nc.gpsimd
            p.memset(ident[:, :], 0.0).then_inc(consts, 1)
            p.memset(ones[:, :], 1.0)
            p.memset(mean1[:, :], 1.0 / D)
            p.memset(three_halves[:, :], 1.5)
            for i in range(2):
                last = p.memset(vaug[i][:, :, :, DH:VW], 0.0)
            last.then_inc(consts, 1)
            pool.wait_ge(consts, 2)
            p.affine_select(out=ident[:, :], in_=ident[:, :], compare_op=ALU.not_equal, fill=1.0, base=0,
                            pattern=[[-1, P]], channel_multiplier=1).then_inc(consts, 1)
            pool.wait_ge(consts, 3)
            p.tensor_copy(identb[:, :], ident[:, :]).then_inc(consts, 1)
            for i in range(2):
                last = p.memset(vaug[i][:, :, :, DH:DH + 1], 1.0)
            last.then_inc(consts, 1)

            def xb(n):
                return X[:, bass.ds(n, 1), :, :].rearrange("p o c t -> p (o c) t")

            def low_q(st, parts, hi_at, lo_at, mid, low):
                n = st.n(2)
                after(pool, mid, n + 1)
                p.tensor_tensor(parts[:, lo_at, :, :], rest[:, :, :], parts[:, 1, :, :],
                                ALU.subtract).then_inc(low, 1)

            def newton_steps(st):
                done = NEWTON_OPS * st.n(3)
                c = slice(0 if st.L["N"] == 0 else 2, 4 if st.L["C"] is not None else 2)
                r, t = rstd[:, c], tmp4[:, c]
                after(pool, guess_ready, st.n(3) + 1)
                for i in range(3):
                    after(pool, newton, done + 4 * i)
                    p.tensor_tensor(t, r, r, ALU.mult).then_inc(newton, 1)
                    after(pool, newton, done + 4 * i + 1)
                    p.tensor_tensor(t, t, half_var[:, c], ALU.mult).then_inc(newton, 1)
                    after(pool, newton, done + 4 * i + 2)
                    p.tensor_tensor(t, t, three_halves[:, c], ALU.add).then_inc(newton, 1)
                    after(pool, newton, done + 4 * i + 3)
                    p.tensor_tensor(r, r, t, ALU.mult).then_inc(newton, 1)

            def step(st):
                L = st.L
                for g in range(SLOTS):
                    if g == 0 and L["C3"] is not None:
                        h_low_part(st.n(-3), HC - 1)
                    if g == 2:
                        if L["C"] is not None:
                            b, k = st.bank("Wo")
                            after(pool, work_free[b], k + 1)
                            b, k = st.last().bank("bcN" if st.last().L["N"] == 0 else "bcC")
                            after(pool, work_full[b], k + 1)
                            p.tensor_tensor(dg[:, :, :].rearrange("p (c u) t -> p c (u t)", c=FC),
                                            y[:, :, :], y[:, :, :], ALU.mult).then_inc(sq_c, 1)
                        if L["N"] == 0:
                            n = st.n(3)
                            after(pool, x_loaded, 16 * (n + 1))
                            after(pool, n_lo, n)
                            p.tensor_tensor(nrm[:, :, :], xb(n), xb(n), ALU.mult).then_inc(sq_n, 1)
                        if L["A"] is not None:
                            low_q(st, qp, 0, 2, q_mid, q_low)
                    if g == 3 and L["A"] is not None:
                        low_q(st, kp, 2, 0, k_mid, k_low)
                    if g == 4 and (L["N"] == 0 or L["C"] is not None):
                        newton_steps(st)
                    if g == 5:
                        if L["C"] == 0:
                            n = st.n(-1)
                            p.tensor_tensor(xb(n), xb(n), y[:, :, :], ALU.add).then_inc(z_ready, 1)
                        if L["N"] == 1:
                            n = st.n(3)
                            after(pool, n_hi, n + 1)
                            if L["V"] is not None:
                                b, k = st.bank("V")
                                after(pool, work_full[b], k + 1)
                            p.tensor_tensor(xnl[1 - st.par][:, :, :], xb(n - B),
                                            xnh[1 - st.par][:, :, :].bitcast(F32), ALU.subtract).then_inc(n_lo, 1)
                    if L["C2"] is not None and g >= 1:
                        h_low_part(st.n(-2), g - 1)
                if L["C"] == 0:
                    after(pool, c_hi, st.n(-1) + 1)
                    p.tensor_tensor(xcl[1 - st.par][:, :, :], crm[:, :, :],
                                    xch[1 - st.par][:, :, :].bitcast(F32), ALU.subtract).then_inc(c_lo, 1)
                if L["C"] == 1:
                    n = st.n(-1)
                    after(pool, c_affine, 2 * (n + 1))
                    p.tensor_tensor(crm[:, :, :], crm[:, :, :], xb(n - B), ALU.add).then_inc(out_ready, 1)
                if L["N"] == 0:
                    after(pool, n_hi, st.n(3) + 1)
                    p.tensor_tensor(xnl[1 - st.par][:, :, :], nrm[:, :, :],
                                    xnh[1 - st.par][:, :, :].bitcast(F32), ALU.subtract).then_inc(n_lo, 1)

            def h_low_part(n, i):
                after(pool, h_high, HC * n + i + 1)
                after(pool, down_done, HC * n + i - 1)
                p.tensor_tensor(hl[:, i % 2, :], hf[:, i % 2, :], hh[:, i % 2, :].bitcast(F32),
                                ALU.subtract).then_inc(h_low, 1)

            run_steps(nc.gpsimd, step)


def kernel(**inputs):
    import numpy as np
    import concourse.bacc as bacc
    from concourse.bass_utils import run_bass_kernel_spmd

    a = {k: np.asarray(v) for k, v in inputs.items()}

    def t(name):
        return a[name].T

    def chunks(vec):
        return vec.reshape(-1, P).T

    def words(m):
        return np.ascontiguousarray(m).view(np.int32).reshape(TC, P, T // 4).transpose(1, 0, 2)

    arrays = {
        "xT": a["x"].transpose(2, 0, 1).reshape(FC, P, B * T),
        "w0": np.stack([t("L0_cond_Wq"), t("L0_cond_Wk"), t("L0_cond_Wv"), t("L0_cond_Wo")]),
        "w_ffn": np.stack([t("L0_cond_gate_w"), t("L0_cond_hid_w")]),
        "w_out": t("L0_cond_out_w"),
        "w1": np.stack([t("L1_cond_Wq"), t("L1_cond_Wk"), t("L1_cond_Wv"), t("L1_cond_Wo")]),
        "condT": t("cond_256"),
        "cond_w": np.concatenate([t("L0_cond_g1w"), t("L0_cond_b1w"), t("L0_cond_g2w"), t("L0_cond_b2w"),
                                  t("L1_cond_Wc")], axis=1),
        "cond_b": chunks(np.concatenate([a["L0_cond_g1b"], a["L0_cond_b1b"], a["L0_cond_g2b"],
                                         a["L0_cond_b2b"], a["L1_cond_bc"]])),
        "rms_scale": chunks(a["L1_cond_rms_scale"]),
        "mask": words(a["mask_SxS_bk1"]),
        "maskT": words(a["mask_SxS_bk1"].T),
    }
    arrays = {k: np.ascontiguousarray(v) for k, v in arrays.items()}
    nc = bacc.Bacc("TRN2", target_bir_lowering=False, num_devices=1)
    args = [nc.dram_tensor(k, v.shape, mybir.dt.from_np(v.dtype), kind="ExternalInput").ap()
            for k, v in arrays.items()]
    args.append(nc.dram_tensor("yT", (FC, P, B * T), F32, kind="ExternalOutput").ap())
    build(nc, *args)
    r = run_bass_kernel_spmd(nc, [arrays], core_ids=[0])
    out = np.asarray(r.results[0]["yT"])
    return np.ascontiguousarray(out.reshape(D, B, T).transpose(1, 2, 0))
```

```python
from contextlib import ExitStack

import concourse.bass as bass
from concourse import mybir

F32 = mybir.dt.float32
F32R = mybir.dt.float32r
BF16 = mybir.dt.bfloat16
I32 = mybir.dt.int32
U8 = mybir.dt.uint8
ACT = mybir.ActivationFunctionType
ALU = mybir.AluOpType
AX_X = mybir.AxisListType.X

P = 128
B = 16
T = 256
D = 256
H = 16
DH = D // H
HID = 1024
FC = D // P
TC = T // P
HC = HID // P
DT = 64
EPS = 1e-6
SCORE_SCALE = DH ** -0.5
PARTS = 6 * DH
MASKED = PARTS + 1
ROWS = MASKED + 3
SLOTS = 8
UNITS = 16
E_RING = 8
VW = 32
NEG = -1.0e38
VAR_TOP = 3.0e38
CLAMP = 5.0e37
ONE_PAIR = 1 + 0x3F80 / 2 ** 23
RSQRT_MAGIC = float(0x5F3759DF)
NEWTON_OPS = 12
BRANCH = B - 1
SHIFT_OPS = 4
FIRST, LAST = -3, 2 * B + 1
SPARE = B + 3

C_G1, C_B1, C_G2, C_B2, C_SHIFT, C_SCALE = 0, 2, 4, 6, 8, 10
CCH = 12


def stages(s):
    def layer(n):
        return None if n < 0 or n >= 2 * B else n // B
    at = {"N": s + 3, "A": s + 2, "V": s + 1, "B1": s + 1, "B2": s, "C": s - 1}
    found = {k: layer(n) for k, n in at.items()}
    found["C2"] = 0 if layer(s - 2) == 0 else None
    found["C3"] = 0 if layer(s - 3) == 0 else None
    found["R"] = 1 if layer(s - 2) == 1 else None
    return found


def q_slot(L, later=0):
    return None if L["A"] is None else 1 - L["A"] + later


def bank_uses(L):
    uses = []
    for g in range(SLOTS):
        if g == 0 and L["A"] == 1:
            uses.append("Q")
        if g == 0 and L["B2"] is not None:
            uses.append("sh1")
        if g == 1 and L["C"] is not None:
            uses += ["T1a", "T1b"]
        if g == 1 and L["A"] == 0:
            uses.append("Q")
        if g == 2 and L["C"] is not None:
            uses.append("T2")
        if g == 3 and L["C"] is not None:
            uses.append("Wo")
        if g == q_slot(L, 1):
            uses.append("K")
        if g == 1 and L["R"] is not None:
            uses.append("bcR")
        if g == 3 and L["V"] is not None:
            uses.append("V")
        if g == 5:
            uses += ["ms"] * (L["N"] == 0 or L["C"] is not None) + ["sh0"] * (L["B1"] is not None)
        if L["C2"] is not None:
            uses.append(f"F{g}")
        if g == 6:
            uses += ["bcC"] * (L["C"] == 0) + ["bcN"] * (L["N"] == 0)
    return uses


def turns_of(s):
    uses = bank_uses(stages(s))
    small = [u for u in uses if s >= SPARE and u in ("sh0", "sh1", "bcR")]
    return [u for u in uses if u not in small], small


USES_BEFORE = {FIRST: (0, 0)}
for _s in range(FIRST, LAST + 1):
    USES_BEFORE[_s + 1] = tuple(n + len(u) for n, u in zip(USES_BEFORE[_s], turns_of(_s)))


class Step:

    def __init__(self, s0, turn=None, full=True):
        self.s0, self.turn, self.full = s0, turn, full
        self.par = s0 % 2
        self.L = stages(s0)
        self.s = s0 if turn is None else turn * 2 + s0

    def n(self, ahead):
        return self.s + ahead

    def last(self):
        return Step(self.s0 - 1, self.turn, self.full)

    def bank(self, use):
        in_turn, small = turns_of(self.s0)
        spare = use in small
        at, banks = (small, 1) if spare else (in_turn, 2)
        k = USES_BEFORE[self.s0][spare] + at.index(use)
        before = k // banks
        if self.turn is not None:
            per = (USES_BEFORE[self.s0 + 2][spare] - USES_BEFORE[self.s0][spare]) // banks
            before = self.turn * per + before
        if spare:
            return 2, before
        return k % 2, before


def key_halves(layer, full):
    return (1,) if layer == 1 and not full else (0, 1)


def after(eng, sem, count):
    if isinstance(count, int) and count <= 0:
        return
    eng.wait_ge(sem, count)


def run_steps(eng, step, short=None):
    for s in range(FIRST, 3):
        step(Step(s))
    with eng.Fori(0, 5) as turn:
        step(Step(3, turn))
        step(Step(4, turn))
    for s in range(13, BRANCH):
        step(Step(s))

    def layer_1(full):
        for s in range(BRANCH, 19):
            step(Step(s, full=full))
        with eng.Fori(0, 5) as turn:
            step(Step(19, turn, full))
            step(Step(20, turn, full))
        for s in range(29, LAST + 1):
            step(Step(s, full=full))

    if short is None:
        layer_1(True)
    else:
        with eng.If(short() == 1):
            layer_1(False)
        with eng.Else():
            layer_1(True)


def build(nc, xT, w0, w_ffn, w_out, w1, condT, cond_w, cond_b, rms_scale, mask, maskT, yT):
    ctx = ExitStack()
    with ctx:
        def sb(name, shape, dt):
            return ctx.enter_context(nc.sbuf_tensor(name, shape, dt))

        def pb(name):
            return ctx.enter_context(nc.psum_tensor(name, [P, 512], F32))

        def sem(name):
            return ctx.enter_context(nc.semaphore(name))

        X = sb("X", [P, B, FC, T], F32)
        Wh = sb("Wh", [P, 4, FC, D], F32R)
        Wl = sb("Wl", [P, 4, FC, D], F32R)
        Gh = sb("Gh", [P, 2, FC, HID], F32R)
        Gl = sb("Gl", [P, 2, FC, HID], F32R)
        Uh = sb("Uh", [P, HC, D], F32R)
        Ul = sb("Ul", [P, HC, D], F32R)
        stack = [sb(f"stack{i}", [P, 2, H, T], BF16) for i in range(2)]
        qst = [t[:, 0, :, :] for t in stack]
        kst = [t[:, 1, :, :] for t in stack]
        vaug = [sb(f"vaug{i}", [P, TC, H, VW], F32) for i in range(2)]
        E = sb("E", [P, E_RING, 2 * T], F32)
        nrm = sb("nrm", [P, FC, T], F32)
        xnh = [sb(f"xnh{i}", [P, FC, T], F32R) for i in range(2)]
        xnl = [sb(f"xnl{i}", [P, FC, T], F32R) for i in range(2)]
        dg = sb("dg", [P, 4, P], F32)
        crm = sb("crm", [P, FC, T], F32)
        xch = [sb(f"xch{i}", [P, FC, T], F32R) for i in range(2)]
        xcl = [sb(f"xcl{i}", [P, FC, T], F32R) for i in range(2)]
        rest = sb("rest", [P, FC, T], F32)
        qp = sb("qp", [P, 3, FC, T], BF16)
        kp = sb("kp", [P, 3, FC, T], BF16)
        oT = sb("oT", [P, 4, T], F32)
        on = sb("on", [P, TC, H, DH], F32)
        oh = sb("oh", [P, FC, T], F32R)
        ol = sb("ol", [P, FC, T], F32R)
        y = sb("y", [P, FC, T], F32)
        th = sb("th", [P, 2, T], F32)
        hf = sb("hf", [P, 2, T], F32)
        hh = sb("hh", [P, 2, T], F32R)
        hl = sb("hl", [P, 2, T], F32R)
        msk = sb("msk", [P, TC, T], BF16)
        mskT = sb("mskT", [P, TC, T], BF16)
        ident = sb("ident", [P, P], F32)
        identb = sb("identb", [P, P], BF16)
        ones = sb("ones", [P, P], F32)
        mean1 = sb("mean1", [P, 1], F32)
        cond = sb("cond", [P, CCH, B], F32)
        var = sb("var", [P, 4], F32)
        half_var = sb("half_var", [P, 4], F32)
        three_halves = sb("three_halves", [P, 4], F32)
        half = sb("half", [P, 4], F32)
        rstd = sb("rstd", [P, 4], F32)
        tmp4 = sb("tmp4", [P, 4], F32)
        nmax = sb("nmax", [P, 2, TC, 8], F32)
        nrest = sb("nrest", [P, TC, 8], F32)
        nparts = sb("nparts", [P, TC, 3, 8], BF16)
        rows = sb("rows", [P, T], BF16)
        nT = rows[0:24, :]
        mask_row = rows[32:33, :]
        rsum = sb("rsum", [P, TC, H], F32)
        cT = sb("cT", [DT, 2, B], F32)
        cth = sb("cth", [DT, B], F32)
        cb = sb("cb", [P, CCH], F32)
        rs = sb("rs", [P, FC], F32)
        uneven = sb("uneven", [P, 1], F32)
        hidden = sb("hidden", [P, 1], F32)
        short_f = sb("short_f", [P, 1], F32)
        short_flag = sb("short_flag", [P, 1], I32)

        s1ps = [pb(f"s1ps{i}") for i in range(2)]
        s2ps = [pb(f"s2ps{i}") for i in range(2)]
        pvps = pb("pvps")
        acc = pb("acc")
        work = [pb("work0"), pb("work1"), acc]

        scr = [nc.dram_tensor(f"scr{i}", (2, 6 * DH, 8 * T), BF16, kind="Internal").ap() for i in range(2)]
        m_scr = [nc.dram_tensor(f"m_scr{i}", (24, T), BF16, kind="Internal").ap() for i in range(2)]

        x_loaded = sem("x_loaded")
        raw_loaded = [sem(f"raw_loaded{i}") for i in range(2)]
        small_loaded = sem("small_loaded")
        raw_hi = sem("raw_hi")
        raw_lo = sem("raw_lo")
        swap_loaded = sem("swap_loaded")
        swap_hi = sem("swap_hi")
        swap_lo = sem("swap_lo")
        consts = sem("consts")
        stack_ones = sem("stack_ones")
        setup = sem("setup")
        cond_tanh = sem("cond_tanh")
        cond_silu = sem("cond_silu")
        cond_mm = sem("cond_mm")
        cond_ready = sem("cond_ready")
        masks_ready = sem("masks_ready")
        counts_in, counts_ready, flag_order = sem("counts_in"), sem("counts_ready"), sem("flag_order")
        flag_ready, mask_row_ready = sem("flag_ready"), sem("mask_row_ready")
        mask_row_loaded = [sem(f"mask_row_loaded{i}") for i in range(2)]
        mask_loaded = sem("mask_loaded")
        sq_n = sem("sq_n")
        sq_c = sem("sq_c")
        z_ready = sem("z_ready")
        work_full = [sem(f"work_full{i}") for i in range(3)]
        work_free = [sem(f"work_free{i}") for i in range(3)]
        newton = sem("newton")
        guess_order, guess_ready = sem("guess_order"), sem("guess_ready")
        diag_ready = sem("diag_ready")
        n_affine = sem("n_affine")
        n_hi = sem("n_hi")
        n_lo = sem("n_lo")
        c_affine = sem("c_affine")
        c_hi = sem("c_hi")
        c_lo = sem("c_lo")
        q_high, q_mid, q_low = sem("q_high"), sem("q_mid"), sem("q_low")
        k_high, k_mid, k_low = sem("k_high"), sem("k_mid"), sem("k_low")
        q_written, k_written = sem("q_written"), sem("k_written")
        stack_loaded = [sem(f"stack_loaded{i}") for i in range(2)]
        s1_full, s1_free = sem("s1_full"), sem("s1_free")
        shift_order, shift_parts = sem("shift_order"), sem("shift_parts")
        shift_written = sem("shift_written")
        shift_loaded = [sem(f"shift_loaded{i}") for i in range(2)]
        s2_full, exp_done = sem("s2_full"), sem("exp_done")
        pv_done, oT_ready = sem("pv_done"), sem("oT_ready")
        sums_inv = sem("sums_inv")
        o_high = sem("o_high")
        tanh_ready, silu_ready = sem("tanh_ready"), sem("silu_ready")
        h_high, h_low = sem("h_high"), sem("h_low")
        down_done, x1_ready = sem("down_done"), sem("x1_ready")
        out_ready, out_stored = sem("out_ready"), sem("out_stored")

        raw = [E[:, 4 * i:4 * i + 4, :] for i in range(2)]
        RAW = [
            (w0.rearrange("w (c p) n -> p (w c) n", p=P), Wh[:, :, :, :].rearrange("p w c n -> p (w c n)"),
             Wl[:, :, :, :].rearrange("p w c n -> p (w c n)")),
        ] + [
            (w_ffn[i].rearrange("(c p) n -> p c n", p=P), Gh[:, i, :, :].rearrange("p c n -> p (c n)"),
             Gl[:, i, :, :].rearrange("p c n -> p (c n)")) for i in range(2)
        ] + [
            (w_out.rearrange("(c p) n -> p c n", p=P), Uh[:, :, :].rearrange("p c n -> p (c n)"),
             Ul[:, :, :].rearrange("p c n -> p (c n)")),
        ]
        RAW_SPLIT = {FIRST: 1, FIRST + 1: 2, FIRST + 2: 3}
        SWAPS = {(13, 4): 0, (13, 6): 1, (14, 4): 2, (16, 4): 3}

        def flat(ap):
            return ap.rearrange("p a b -> p (a b)")

        block = ctx.enter_context(nc.Block())

        @block.sync
        def _(sp):
            def load_x(n):
                sp.dma_start(X[:, bass.ds(n, 1), :, :].rearrange("p o c t -> p (o c) t"),
                             xT[:, :, bass.ds(n * T, T)].rearrange("c p t -> p c t")).then_inc(x_loaded, 16)

            def load_raw(i):
                src = RAW[i][0]
                if i >= 2:
                    after(sp, raw_lo, i - 1)
                sp.dma_start(raw[i % 2].rearrange("p a b -> p (a b)").rearrange(
                    "p (c n) -> p c n", c=src.shape[1]), src).then_inc(raw_loaded[i % 2], 16)

            load_x(0)
            for dst, s in ((cT[:, 0, :], condT), (cb[:, :], cond_b), (rs[:, :], rms_scale)):
                sp.dma_start(dst, s).then_inc(small_loaded, 16)
            for i, buf in enumerate((y, rest, crm)):
                sp.dma_start(flat(buf[0:DT, :, :]), cond_w[:, 512 * i:512 * (i + 1)]).then_inc(small_loaded, 16)
            load_raw(0)
            for i, src in enumerate((mask, maskT)):
                sp.dma_start(hf[:, i, 0:P].bitcast(I32).rearrange("p (c t) -> p c t", c=TC), src)\
                  .then_inc(mask_loaded, 16)
            load_raw(1)
            load_raw(2)

            def write_parts(par, row, parts, written):
                for c in range(FC):
                    dst = bass.AP(scr[par].tensor, (6 * DH * c + row) * 8 * T,
                                  [[T, P], [DH * 8 * T, 3], [1, T]])
                    sp.dma_start(dst, parts[:, :, c, :]).then_inc(written, 16)

            def read_stack(par, half_):
                row = 0
                for parts in (3, 2, 1):
                    k = DH * parts
                    src = bass.AP(scr[par].tensor, half_ * 6 * DH * 8 * T,
                                  [[8 * T, k], [(6 * DH - k) * 8 * T, 2], [1, 8 * T]])
                    dst = stack[par][row:row + k, :, 8 * half_:8 * half_ + 8, :]
                    sp.dma_start(dst.rearrange("r o h t -> r o (h t)"), src).then_inc(stack_loaded[half_], 16)
                    row += k

            def store_result(n, made):
                after(sp, out_ready, made)
                sp.dma_start(yT[:, :, bass.ds(n * T, T)].rearrange("c p t -> p c t"), crm[:, :, :])\
                  .then_inc(out_stored, 16)

            def mask_row_in(st, half_):
                if st.s0 in (BRANCH - 1, BRANCH):
                    sp.wait_ge(mask_row_ready, 1)
                    sp.dma_start(kst[st.par][PARTS:MASKED, 8 * half_:8 * half_ + 8, :],
                                 mask_row[:, None, :].to_broadcast([1, 8, T])).then_inc(mask_row_loaded[half_], 16)

            def step(st):
                L, par = st.L, st.par

                registers = []

                def held(count):
                    if isinstance(count, int):
                        return count
                    registers.append(nc.sync.alloc_register(f"held{st.s0}_{len(registers)}"))
                    nc.sync.reg_mov(registers[-1], count)
                    return nc.sync.snap(registers[-1], min_val=0, max_val=1 << 20)

                n_x, n_a, n_b1, n_b2 = st.n(3), st.n(2), st.n(1), st.n(0)
                x_before = held(16 * n_x)
                scratch_read = held(48 * (n_a - 1))
                a_split = held(n_a + 1)
                a_written = held(32 * (n_a + 1))
                heads_used = [held(UNITS * n_b2 + 8), held(UNITS * n_b2 + 16)]
                rows_used = [held(UNITS * n_b2), held(UNITS * (n_b2 - 1))]
                rows_read = [held(16 * n_b1), held(16 * n_b2)]
                rows_written = [held(16 * (2 * n_b1 + 1)), held(16 * (2 * n_b2 + 2))]
                rows_made = [None, None]
                for half_, stage in enumerate(("B1", "B2")):
                    if L[stage] is not None:
                        b, k = st.bank(f"sh{half_}")
                        rows_made[half_] = (work_free[b], held(k + 1))
                result_made = held(st.n(-2 - B) + 1)

                def rows_out(half_):
                    after(sp, shift_loaded[half_], rows_read[half_])
                    after(sp, *rows_made[half_])
                    sp.dma_start(m_scr[half_], nT).then_inc(shift_written, 16)

                def rows_in(half_):
                    after(sp, s2_full, rows_used[half_])
                    after(sp, shift_written, rows_written[half_])
                    sp.dma_start(qst[par if half_ else 1 - par][MASKED:ROWS, 8 * half_:8 * half_ + 8, :],
                                 m_scr[half_].rearrange("(r h) t -> r h t", r=3)).then_inc(shift_loaded[half_], 16)

                def load_swap(slot):
                    m = SWAPS.get((st.s0, slot))
                    if m is not None:
                        after(sp, swap_lo, m)
                        if m == 0:
                            sp.wait_ge(n_lo, B)
                            sp.wait_ge(n_hi, B)
                        sp.dma_start(nrm[:, :, :], w1[m].rearrange("(c p) n -> p c n", p=P)).then_inc(swap_loaded, 16)

                if L["N"] == 0 and st.s0 > FIRST:
                    after(sp, x_loaded, x_before)
                    load_x(n_x)
                if st.s0 == FIRST + 1:
                    load_raw(3)
                load_swap(4)
                if L["B2"] is not None:
                    rows_out(1)
                    rows_in(1)
                if L["A"] is not None:
                    for half_ in range(2):
                        after(sp, stack_loaded[half_], scratch_read)
                    after(sp, q_low, a_split)
                    write_parts(par, 0, qp, q_written)
                    after(sp, k_low, a_split)
                    write_parts(par, 3 * DH, kp, k_written)
                    after(sp, q_written, a_written)
                    after(sp, k_written, a_written)
                    if L["B2"] is not None:
                        after(sp, s2_full, heads_used[0])
                    mask_row_in(st, 0)
                    read_stack(par, 0)
                load_swap(6)
                if L["R"] is not None:
                    store_result(st.n(-2 - B), result_made)
                if L["B1"] is not None:
                    rows_out(0)
                    rows_in(0)
                if L["A"] is not None:
                    if L["B2"] is not None:
                        after(sp, s2_full, heads_used[1])
                    mask_row_in(st, 1)
                    read_stack(par, 1)
                for r in registers:
                    nc.sync.free_register(r)

            run_steps(nc.sync, step)
            sp.wait_ge(out_stored, 16 * B)

        @block.tensor
        def _(pe):
            mm = nc.tensor.matmul

            def mm3(out, lh, ll, rh, rl, first, last):
                mm(out, lh, rh, start=first, stop=False, skip_group_check=True)
                mm(out, lh, rl, start=False, stop=False, skip_group_check=True)
                return mm(out, ll, rh, start=False, stop=last, skip_group_check=True)

            pe.wait_ge(small_loaded, 16 * 6)
            pe.wait_ge(cond_silu, 1)
            for c in range(CCH):
                src = (y, rest, crm)[c // 4][0:DT, :, :].rearrange("p a b -> p (a b)")
                last = mm(acc[:, B * c:B * (c + 1)], src[:, P * (c % 4):P * (c % 4 + 1)],
                          cT[:, 0 if c < 8 else 1, :], start=True, stop=True)
            last.then_inc(cond_mm, 1)

            def open_bank(st, use):
                b, k = st.bank(use)
                after(pe, work_free[b], k)
                return work[b], work_full[b]

            def project_T(out, w, xh, xl, chunks=FC):
                for m in range(FC):
                    for c in range(chunks):
                        last = mm3(out[:, m * T:(m + 1) * T], Wh[:, w, c, P * m:P * (m + 1)],
                                   Wl[:, w, c, P * m:P * (m + 1)], xh[:, c, :], xl[:, c, :],
                                   c == 0, c == chunks - 1)
                return last

            def scores_for_max(st, g):
                n, par = st.n(1), 1 - st.par
                if g in (0, 4):
                    after(pe, stack_loaded[g // 4], 48 * (n + 1))
                    if st.s0 in (BRANCH, BRANCH + 1):
                        pe.wait_ge(mask_row_loaded[g // 4], 16 * (st.s0 - BRANCH + 1))
                if not st.full:
                    before = 1 if g == 0 and st.s0 == BRANCH else 2
                    after(pe, s1_free, UNITS * n + 2 * g - before)
                    bank = s1ps[g % 2]
                    for qh in range(TC):
                        out = bank[:, T * qh:T * (qh + 1)]
                        for i in range(2):
                            h = 2 * g + i
                            last = mm(out[:, P * i:P * (i + 1)], qst[par][0:MASKED, h, P * qh:P * (qh + 1)],
                                      kst[par][0:MASKED, h, P:T], start=True, stop=True,
                                      skip_group_check=True)
                    last.then_inc(s1_full, 2)
                    return
                for qh in range(TC):
                    u = 2 * g + qh
                    after(pe, s1_free, UNITS * n + u - 1)
                    bank = s1ps[u % 2]
                    if st.L["B1"] == 1:
                        mm(bank[:, :].rearrange("p (h t) -> p h t", h=2), identb[:, :],
                           msk[:, qh, :][:, None, :].to_broadcast([P, 2, T]),
                           start=True, stop=False, skip_group_check=True)
                    for i in range(2):
                        h = 2 * g + i
                        last = mm(bank[:, T * i:T * (i + 1)], qst[par][0:PARTS, h, P * qh:P * (qh + 1)],
                                  kst[par][0:PARTS, h, :], start=st.L["B1"] == 0, stop=True,
                                  skip_group_check=True)
                    last.then_inc(s1_full, 1)

            def scores(st, g):
                n, par = st.n(0), st.par
                if g in (0, 4):
                    after(pe, shift_loaded[g // 4], 16 * (n + 1))
                short = st.L["B2"] == 1 and not st.full
                for kh in key_halves(st.L["B2"], st.full):
                    u = 2 * g + kh
                    before = 1 if g == 0 and st.s0 == BRANCH + 1 else 2
                    after(pe, exp_done, UNITS * n + (2 * g - before if short else u - 1))
                    bank = s2ps[g % 2 if short else u % 2]
                    add_mask = st.L["B2"] == 1 and st.full
                    if add_mask:
                        mm(bank[:, :].rearrange("p (h t) -> p h t", h=2), identb[:, :],
                           mskT[:, kh, :][:, None, :].to_broadcast([P, 2, T]),
                           start=True, stop=False, skip_group_check=True)
                    for i in range(2):
                        h = 2 * g + i
                        last = mm(bank[:, T * i:T * (i + 1)], kst[par][0:ROWS, h, P * kh:P * (kh + 1)],
                                  qst[par][0:ROWS, h, :], start=not add_mask, stop=True,
                                  skip_group_check=True)
                    last.then_inc(s2_full, 2 if short else 1)

            def values(st, j):
                n, layer = (st.n(-1), st.L["C"]) if j == 3 else (st.n(0), st.L["B2"])
                halves = key_halves(layer, st.full)
                v_of = vaug[st.par if j < 3 else 1 - st.par]
                after(pe, exp_done, UNITS * n + 4 * j + 4)
                if j % 2 == 0:
                    after(pe, oT_ready, 2 * n + j // 2)
                for kh in halves:
                    for i in range(4):
                        h = 4 * j + i
                        u = 2 * (h // 2) + kh
                        last = mm(pvps[32 * i:32 * (i + 1), T * (j % 2):T * (j % 2 + 1)],
                                  v_of[:, kh, h, :], E[:, u % E_RING, T * (h % 2):T * (h % 2 + 1)],
                                  start=kh == halves[0], stop=kh == TC - 1, skip_group_check=True)
                last.then_inc(pv_done, 1)

            def swiglu_up(st, i):
                bank, full = open_bank(st, f"F{i}")
                if i == 0:
                    after(pe, c_lo, st.n(-2) + 1)
                for w in range(2):
                    for c in range(FC):
                        last = mm3(bank[:, T * w:T * (w + 1)], Gh[:, w, c, P * i:P * (i + 1)],
                                   Gl[:, w, c, P * i:P * (i + 1)], xch[st.par][:, c, :],
                                   xcl[st.par][:, c, :], c == 0, c == FC - 1)
                last.then_inc(full, 1)

            def swiglu_down(n, i):
                after(pe, h_low, HC * n + i + 1)
                if i == 0:
                    after(pe, x1_ready, n)
                for m in range(FC):
                    last = mm3(acc[:, T * m:T * (m + 1)], Uh[:, i, P * m:P * (m + 1)],
                               Ul[:, i, P * m:P * (m + 1)], hh[:, i % 2, :], hl[:, i % 2, :],
                               i == 0 and m == 0, i == HC - 1)
                last.then_inc(down_done, 1)

            def divide_in(st):
                after(pe, oT_ready, 2 * st.n(-1) + 2)
                for qh, use in enumerate(("T1a", "T1b")):
                    bank, full = open_bank(st, use)
                    for j in range(4):
                        last = nc.tensor.transpose(bank[:, P * j:P * (j + 1)], oT[:, j, P * qh:P * (qh + 1)],
                                                   ident[:, :])
                    last.then_inc(full, 1)

            def divide_out(st):
                for use in ("T1a", "T1b"):
                    b, k = st.bank(use)
                    after(pe, work_free[b], k + 1)
                bank, full = open_bank(st, "T2")
                for m in range(FC):
                    for qh in range(TC):
                        src = on[:, qh, 8 * m:8 * m + 8, :].rearrange("p h d -> p (h d)")
                        last = nc.tensor.transpose(bank[:, T * m + P * qh:T * m + P * (qh + 1)], src,
                                                   ident[:, :])
                last.then_inc(full, 1)

            def value_projection(st):
                n = st.n(1)
                par = 1 - st.par
                after(pe, n_lo, n + 1)
                bank, full = open_bank(st, "V")
                for t in range(TC):
                    for c in range(FC):
                        last = mm3(bank[:, D * t:D * (t + 1)], xnh[par][:, c, P * t:P * (t + 1)],
                                   xnl[par][:, c, P * t:P * (t + 1)], Wh[:, 2, c, :], Wl[:, 2, c, :],
                                   c == 0, c == FC - 1)
                last.then_inc(full, 1)

            def output_projection(st):
                b, k = st.bank("T2")
                after(pe, work_free[b], k + 1)
                bank, full = open_bank(st, "Wo")
                project_T(bank, 3, oh, ol).then_inc(full, 1)

            def qk_projection(st, use, w):
                after(pe, n_lo, st.n(2) + 1)
                bank, full = open_bank(st, use)
                project_T(bank, w, xnh[st.par], xnl[st.par]).then_inc(full, 1)

            def mean_squares(st):
                bank, full = open_bank(st, "ms")
                jobs = []
                if st.L["N"] == 0:
                    after(pe, sq_n, st.n(3) + 1)
                    jobs.append((nrm[:, :, :], 0))
                if st.L["C"] is not None:
                    after(pe, sq_c, st.n(-1) + 1)
                    jobs.append((dg[:, :, :].rearrange("p (c u) t -> p c (u t)", c=FC), 2))
                for src, col in jobs:
                    for t in range(TC):
                        for c in range(FC):
                            last = mm(bank[:, col + t:col + t + 1], src[:, c, P * t:P * (t + 1)],
                                      mean1[:, :], start=c == 0, stop=c == FC - 1, skip_group_check=True)
                last.then_inc(full, 1)

            def broadcast_rstd(st, use, col):
                bank, full = open_bank(st, use)
                after(pe, diag_ready, st.n(2 if use == "bcR" else 3) + 1)
                mm(bank[:, 0:T], ones[:, :], dg[:, col:col + 2, :].rearrange("p a b -> p (a b)"),
                   start=True, stop=True).then_inc(full, 1)

            def shift_transpose(st, half_):
                bank, full = open_bank(st, f"sh{half_}")
                after(pe, shift_parts, 2 * st.n(1 - half_) + half_ + 1)
                out = bank[0:24, 0:P].bitcast(BF16)
                for qh in range(TC):
                    last = nc.tensor.transpose(out[:, P * qh:P * (qh + 1)],
                                               nparts[:, qh, :, :].rearrange("p r h -> p (r h)"), identb[:, :])
                last.then_inc(full, 1)

            def count_hidden():
                pe.wait_ge(counts_in, 1)
                pe.wait_ge(cond_ready, 2)
                for qh in range(TC):
                    last = mm(acc[:, 0:T], ones[:, :], th[:, qh, :], start=qh == 0, stop=qh == TC - 1)
                last.then_inc(counts_ready, 1)

            def query_projection(st):
                if st.s0 + 2 == B:
                    pe.wait_ge(swap_lo, 2)
                qk_projection(st, "Q", 0)

            def step(st):
                L = st.L
                if st.s0 == FIRST:
                    pe.wait_ge(consts, 5)
                if st.s0 == FIRST + 1:
                    count_hidden()
                    pe.wait_ge(raw_lo, 1)
                if st.s0 == 0:
                    pe.wait_ge(stack_ones, 6)
                if st.s0 == 2:
                    pe.wait_ge(raw_lo, 4)
                if st.s0 == BRANCH:
                    pe.wait_ge(masks_ready, 2)
                if st.s0 == SPARE:
                    pe.wait_ge(x1_ready, B)
                for g in range(SLOTS):
                    if L["C"] is not None:
                        if g == 1:
                            divide_in(st)
                        if g == 2:
                            divide_out(st)
                    if g == 5:
                        if L["N"] == 0 or L["C"] is not None:
                            mean_squares(st)
                        if L["B1"] is not None and st.s0 < SPARE:
                            shift_transpose(st, 0)
                    if g == 0 and L["A"] == 1:
                        query_projection(st)
                    if g == 0 and L["C"] is not None:
                        values(st, 3)
                    if L["B1"] is not None:
                        scores_for_max(st, g)
                    if L["B2"] is not None:
                        if g == 0:
                            shift_transpose(st, 1)
                        scores(st, g)
                        if g in (2, 4, 6):
                            values(st, g // 2 - 1)
                    if g == 4 and L["B1"] is not None and st.s0 >= SPARE:
                        shift_transpose(st, 0)
                    if g == 3 and L["C"] is not None:
                        if st.s0 - 1 == B:
                            pe.wait_ge(swap_lo, 4)
                        output_projection(st)
                    if g == 1 and L["A"] == 0:
                        query_projection(st)
                    if g == q_slot(L, 1):
                        qk_projection(st, "K", 1)
                    if g == 1 and L["R"] is not None:
                        broadcast_rstd(st, "bcR", 2)
                    if g == 3 and L["V"] is not None:
                        if st.s0 + 1 == B:
                            pe.wait_ge(swap_lo, 3)
                        value_projection(st)
                    if L["C2"] is not None:
                        swiglu_up(st, g)
                        if g >= 2:
                            swiglu_down(st.n(-2), g - 2)
                    if g < 2 and L["C3"] is not None:
                        swiglu_down(st.n(-3), HC - 2 + g)
                    if g == 6:
                        if L["C"] == 0:
                            broadcast_rstd(st, "bcC", 2)
                        if L["N"] == 0:
                            broadcast_rstd(st, "bcN", 0)
            def short():
                pe.wait_ge(flag_ready, 1)
                return nc.tensor.value_load(short_flag[0:1, 0:1], min_val=0, max_val=1)

            run_steps(nc.tensor, step, short)

        @block.vector
        def _(dve):
            v = nc.vector

            def raw_low(i):
                _, hi, lo = RAW[i]
                dve.wait_ge(raw_loaded[i % 2], 16 * (i // 2 + 1))
                dve.wait_ge(raw_hi, i + 1)
                v.tensor_tensor(lo, flat(raw[i % 2]), hi.bitcast(F32), ALU.subtract).then_inc(raw_lo, 1)

            dve.wait_ge(cond_tanh, 1)
            v.tensor_scalar(cth[:, :], cth[:, :], 0.5, 0.5, ALU.mult, ALU.add).then_inc(setup, 1)
            dve.wait_ge(setup, 1)
            v.tensor_tensor(cT[:, 1, :], cth[:, :], cT[:, 0, :], ALU.mult).then_inc(cond_silu, 1)
            raw_low(0)

            def conditioning():
                dve.wait_ge(cond_mm, 1)
                v.tensor_tensor(cond[:, :, :], acc[:, 0:CCH * B].rearrange("p (c b) -> p c b", c=CCH),
                                cb[:, :][:, :, None].to_broadcast([P, CCH, B]), ALU.add).then_inc(setup, 1)
                dve.wait_ge(setup, 2)
                for c in range(FC):
                    v.tensor_scalar(cond[:, C_SCALE + c, :], cond[:, C_SCALE + c, :], 1.0,
                                    rs[:, c:c + 1], ALU.add, ALU.mult).then_inc(cond_ready, 1)

            def masks_and_path():
                dve.wait_ge(mask_loaded, 32)
                raw_mask, raw_maskT = (hf[:, i, 0:P].bitcast(U8).rearrange("p (c t) -> p c t", c=TC) for i in range(2))
                v.tensor_scalar(th[:, :, :], raw_mask, 1.0, None, ALU.mult).then_inc(counts_in, 1)
                v.tensor_scalar(msk[:, :, :], raw_mask, NEG, None, ALU.mult).then_inc(masks_ready, 1)
                v.tensor_scalar(mskT[:, :, :], raw_maskT, NEG, None, ALU.mult).then_inc(masks_ready, 1)
                dve.wait_ge(counts_ready, 1)
                v.tensor_copy(y[:, 1, :], acc[:, 0:T]).then_inc(flag_order, 1)
                dve.wait_ge(flag_order, 1)
                v.tensor_reduce(hidden[:, :], y[:, 1, 0:P], AX_X, ALU.add).then_inc(flag_order, 1)
                v.scalar_tensor_tensor(y[:, 0, :], y[:, 1, :], -float(T), y[:, 1, :], ALU.add, ALU.mult)\
                 .then_inc(flag_order, 1)
                dve.wait_ge(flag_order, 3)
                v.tensor_reduce(uneven[:, :], y[:, 0, :], AX_X, ALU.add).then_inc(flag_order, 1)
                dve.wait_ge(flag_order, 4)
                v.tensor_scalar(short_f[:, :], uneven[:, :], -0.5, None, ALU.is_ge).then_inc(flag_order, 1)
                dve.wait_ge(flag_order, 5)
                v.scalar_tensor_tensor(short_f[:, :], hidden[:, :], T * P - 0.5, short_f[:, :], ALU.is_ge, ALU.mult)\
                 .then_inc(flag_order, 1)
                dve.wait_ge(flag_order, 6)
                v.tensor_copy(short_flag[:, :], short_f[:, :]).then_inc(flag_ready, 1)
                dve.wait_ge(masks_ready, 2)
                v.tensor_scalar(mask_row, msk[32:33, 0, :], short_f[32:33, :], None, ALU.mult).then_inc(mask_row_ready, 1)


            def maxima(st, g):
                n = st.n(1)
                if not st.full:
                    after(dve, s1_full, UNITS * n + 2 * g + 2)
                    v.tensor_reduce(nmax[:, g // 4, :, 2 * (g % 4):2 * (g % 4) + 2],
                                    s1ps[g % 2][:, :].rearrange("p (q h t) -> p q h t", q=2, h=2), AX_X,
                                    ALU.max, negate=True).then_inc(s1_free, 2)
                    return
                for qh in range(TC):
                    u = 2 * g + qh
                    after(dve, s1_full, UNITS * n + u + 1)
                    v.tensor_reduce(nmax[:, g // 4, qh, 2 * (g % 4):2 * (g % 4) + 2],
                                    s1ps[u % 2][:, :].rearrange("p (h t) -> p h t", h=2), AX_X, ALU.max,
                                    negate=True).then_inc(s1_free, 1)

            def shift_split(st, half_):
                n = st.n(1)
                k = 2 * n + half_
                done = SHIFT_OPS * k
                nm = nmax[:, half_, :, :]
                after(dve, s1_free, UNITS * n + 8 * half_ + 8)
                v.tensor_scalar(nm, nm, CLAMP, None, ALU.min).then_inc(shift_order, 1)
                after(dve, shift_order, done + 1)
                if half_ or st.L["B2"] is not None:
                    b, k = st.bank("sh0" if half_ else "sh1")
                    after(dve, work_full[b], k + 1)
                v.tensor_copy(nparts[:, :, 0, :], nm).then_inc(shift_order, 1)
                after(dve, shift_order, done + 2)
                v.tensor_tensor(nrest[:, :, :], nm, nparts[:, :, 0, :], ALU.subtract).then_inc(shift_order, 1)
                after(dve, shift_order, done + 3)
                v.tensor_copy(nparts[:, :, 1, :], nrest[:, :, :]).then_inc(shift_order, 1)
                after(dve, shift_order, done + 4)
                v.tensor_tensor(nparts[:, :, 2, :], nrest[:, :, :], nparts[:, :, 1, :],
                                ALU.subtract).then_inc(shift_parts, 1)

            def opened(st, use):
                b, k = st.bank(use)
                after(dve, work_full[b], k + 1)
                return work[b], work_free[b]

            def divide(st):
                for qh, use in enumerate(("T1a", "T1b")):
                    bank, free = opened(st, use)
                    heads = bank[:, :].rearrange("p (h w) -> p h w", w=VW)
                    v.reciprocal(rsum[:, qh, :], heads[:, :, DH]).then_inc(sums_inv, 1)
                    after(dve, sums_inv, TC * st.n(-1) + qh + 1)
                    v.tensor_tensor(on[:, qh, :, :], heads[:, :, 0:DH],
                                    rsum[:, qh, :][:, :, None].to_broadcast([P, H, DH]), ALU.mult)\
                     .then_inc(free, 1)

            def o_split(st):
                bank, free = opened(st, "T2")
                after(dve, o_high, st.n(-1) + 1)
                v.tensor_tensor(flat(ol[:, :, :]), bank[:, :], flat(oh[:, :, :]).bitcast(F32), ALU.subtract)\
                 .then_inc(free, 1)

            def qk_split(st, use, parts, hi_at, high, mid, low):
                n = st.n(2)
                bank, free = opened(st, use)
                after(dve, high, n + 1)
                after(dve, k_low if use == "Q" else q_low, n if use == "Q" else n + 1)
                v.tensor_tensor(flat(rest[:, :, :]), bank[:, :],
                                parts[:, hi_at, :, :].rearrange("p c t -> p (c t)"), ALU.subtract).then_inc(free, 1)
                b, k = st.bank(use)
                after(dve, work_free[b], k + 1)
                v.tensor_copy(parts[:, 1, :, :], rest[:, :, :]).then_inc(mid, 1)

            def attention_residual(st):
                n = st.n(-1)
                bank, free = opened(st, "Wo")
                after(dve, z_ready, n)
                v.tensor_tensor(flat(y[:, :, :]), bank[:, :],
                                X[:, bass.ds(n, 1), :, :].rearrange("p o c t -> p (o c t)"), ALU.add)\
                 .then_inc(free, 1)

            def rsqrt(st):
                lo = 0 if st.L["N"] == 0 else 2
                hi = 4 if st.L["C"] is not None else 2
                c = slice(lo, hi)
                bank, free = opened(st, "ms")
                v.tensor_scalar(var[:, c], bank[:, c], EPS, VAR_TOP, ALU.add, ALU.min).then_inc(free, 1)
                b, k = st.bank("ms")
                after(dve, work_free[b], k + 1)
                v.tensor_scalar(half_var[:, c], var[:, c], -0.5, None, ALU.mult).then_inc(guess_order, 1)
                v.tensor_scalar(half[:, c].bitcast(I32), var[:, c].bitcast(I32), 1, None,
                                ALU.logical_shift_right).then_inc(guess_order, 1)
                after(dve, guess_order, 2 * st.n(3) + 2)
                v.tensor_scalar(rstd[:, c].bitcast(I32), half[:, c].bitcast(I32), -1.0, RSQRT_MAGIC,
                                ALU.mult, ALU.add).then_inc(guess_ready, 1)

            def diagonals(st):
                lo = 0 if st.L["N"] == 0 else 2
                hi = 4 if st.L["C"] is not None else 2
                c = slice(lo, hi)
                after(dve, newton, NEWTON_OPS * (st.n(3) + 1))
                v.tensor_tensor(dg[:, c, :], ident[:, :][:, None, :].to_broadcast([P, hi - lo, P]),
                                rstd[:, c][:, :, None].to_broadcast([P, hi - lo, P]), ALU.mult)\
                 .then_inc(diag_ready, 1)

            def normalize(st, use, dst, src):
                bank, free = opened(st, use)
                v.tensor_tensor(dst, src, bank[:, 0:T][:, None, :].to_broadcast([P, FC, T]), ALU.mult)\
                 .then_inc(free, 1)

            def swiglu(st, i):
                n = st.n(-2)
                bank, free = opened(st, f"F{i}")
                after(dve, tanh_ready, HC * n + i + 1)
                v.scalar_tensor_tensor(th[:, i % 2, :], th[:, i % 2, :], 1.0, bank[:, 0:T],
                                       ALU.add, ALU.mult).then_inc(silu_ready, 1)
                after(dve, silu_ready, HC * n + i + 1)
                after(dve, h_low, HC * n + i - 1)
                v.scalar_tensor_tensor(hf[:, i % 2, :], th[:, i % 2, :], 0.5, bank[:, T:2 * T],
                                       ALU.mult, ALU.mult).then_inc(free, 1)

            def step(st):
                L = st.L
                if st.s0 == FIRST:
                    dve.wait_ge(consts, 5)
                for g in range(SLOTS):
                    if g == 1 and L["C"] is not None:
                        divide(st)
                    if g == 2:
                        if L["C3"] is not None:
                            n = st.n(-3)
                            after(dve, down_done, HC * (n + 1))
                            x_n = X[:, bass.ds(n, 1), :, :].rearrange("p o c t -> p (o c t)")
                            v.tensor_tensor(x_n, acc[:, :], x_n, ALU.add).then_inc(x1_ready, 1)
                        if L["C"] is not None:
                            o_split(st)
                        if L["R"] is not None:
                            after(dve, out_stored, 16 * (st.n(-2) - B))
                            normalize(st, "bcR", crm[:, :, :], y[:, :, :])
                    if g == 5 and (L["N"] == 0 or L["C"] is not None):
                        rsqrt(st)
                    if g == 7:
                        if L["C"] == 0:
                            normalize(st, "bcC", crm[:, :, :], y[:, :, :])
                        if L["N"] == 0:
                            n = st.n(3)
                            normalize(st, "bcN", nrm[:, :, :],
                                      X[:, bass.ds(n, 1), :, :].rearrange("p o c t -> p (o c) t"))
                    if g == 0 and L["A"] == 1:
                        qk_split(st, "Q", qp, 0, q_high, q_mid, q_low)
                    if L["B1"] is not None:
                        if g == 4 and L["B1"] == 1:
                            shift_split(st, 0)
                        maxima(st, g)
                        if g == 4 and L["B1"] == 0:
                            shift_split(st, 0)
                        if g == 7:
                            shift_split(st, 1)
                    if g == 1 and L["A"] == 0:
                        qk_split(st, "Q", qp, 0, q_high, q_mid, q_low)
                    if g == 3 and L["C"] == 0:
                        attention_residual(st)
                    if g == q_slot(L, 1):
                        qk_split(st, "K", kp, 2, k_high, k_mid, k_low)
                    if (g == 7 and L["C"] == 1) or (g == 6 and (L["N"] == 0 or L["C"] == 0)):
                        diagonals(st)
                    if L["C2"] is not None:
                        swiglu(st, g)
                    m = SWAPS.get((st.s0, g))
                    if m is not None:
                        dve.wait_ge(swap_hi, m + 1)
                        v.tensor_tensor(Wl[:, m, :, :], nrm[:, :, :], Wh[:, m, :, :].bitcast(F32),
                                        ALU.subtract).then_inc(swap_lo, 1)
                    if g == 5 and st.s0 in RAW_SPLIT:
                        if st.s0 == FIRST:
                            conditioning()
                        raw_low(RAW_SPLIT[st.s0])
                if st.s0 == FIRST:
                    masks_and_path()
            def short():
                dve.wait_ge(flag_ready, 1)
                return nc.vector.value_load(short_flag[0:1, 0:1], min_val=0, max_val=1)

            run_steps(nc.vector, step, short)

        @block.scalar
        def _(act):
            a = nc.scalar
            def raw_high(i):
                act.wait_ge(raw_loaded[i % 2], 16 * (i // 2 + 1))
                a.copy(RAW[i][1], flat(raw[i % 2])).then_inc(raw_hi, 1)

            act.wait_ge(small_loaded, 16 * 6)
            a.activation(cth[:, :], cT[:, 0, :], ACT.Tanh, scale=0.5).then_inc(cond_tanh, 1)
            raw_high(0)

            def opened(st, use):
                b, k = st.bank(use)
                after(act, work_full[b], k + 1)
                return work[b], work_free[b]

            def exps(st, g):
                n = st.n(0)
                short = st.L["B2"] == 1 and not st.full
                for kh in key_halves(st.L["B2"], st.full):
                    u = 2 * g + kh
                    after(act, s2_full, UNITS * n + u + 1)
                    after(act, pv_done, 4 * n + u // 4 - 1)
                    a.activation(E[:, u % E_RING, :], s2ps[g % 2 if short else u % 2][:, :], ACT.Exp,
                                 scale=SCORE_SCALE).then_inc(exp_done, 2 if short else 1)

            def store_oT(st, pair):
                n = st.n(-pair)
                after(act, pv_done, 4 * n + 2 * pair + 2)
                if pair == 0 and st.L["C"] is not None:
                    for use in ("T1a", "T1b"):
                        b, k = st.bank(use)
                        after(act, work_full[b], k + 1)
                a.copy(oT[:, 2 * pair:2 * pair + 2, :], pvps[:, :].rearrange("p (j t) -> p j t", j=2))\
                 .then_inc(oT_ready, 1)

            def tanh(st, i):
                bank, _ = opened(st, f"F{i}")
                if i >= 2:
                    b, k = st.bank(f"F{i - 2}")
                    after(act, work_free[b], k + 1)
                a.activation(th[:, i % 2, :], bank[:, 0:T], ACT.Tanh, scale=0.5).then_inc(tanh_ready, 1)

            def h_high_part(st, n, i):
                b, k = st.bank(f"F{i}")
                after(act, work_free[b], k + 1)
                after(act, down_done, HC * n + i - 1)
                a.copy(hh[:, i % 2, :], hf[:, i % 2, :]).then_inc(h_high, 1)

            def affine(st, buf, gain, shift, b, done, count):
                for c in range(FC):
                    a.activation(buf[:, c, :], buf[:, c, :], ACT.Identity,
                                 scale=cond[:, gain + c, bass.ds(b, 1)],
                                 bias=cond[:, shift + c, bass.ds(b, 1)]).then_inc(done, 1)
                after(act, done, count)

            def shift_store(st, half_):
                bank, free = opened(st, f"sh{half_}")
                after(act, shift_written, 16 * (2 * st.n(1 - half_) + half_))
                a.copy(nT, bank[0:24, 0:P].bitcast(BF16)).then_inc(free, 1)

            def query_high(st):
                bank, _ = opened(st, "Q")
                after(act, q_written, 32 * st.n(2))
                a.copy(qp[:, 0, :, :].rearrange("p c t -> p (c t)"), bank[:, :]).then_inc(q_high, 1)

            def step(st):
                L = st.L
                if st.s0 == FIRST:
                    act.wait_ge(cond_ready, 2)
                if st.s0 == 0:
                    act.wait_ge(raw_lo, 4)
                for g in range(SLOTS):
                    if g == 0 and L["C3"] is not None:
                        h_high_part(st.last(), st.n(-3), HC - 1)
                    if g == 2 and L["C"] is not None:
                        bank, _ = opened(st, "T2")
                        a.copy(flat(oh[:, :, :]), bank[:, :]).then_inc(o_high, 1)
                    if g == 0 and L["A"] == 1:
                        query_high(st)
                    if g == 0 and L["C"] is not None:
                        store_oT(st, 1)
                    if g == 5 and st.s0 >= SPARE:
                        if L["B1"] is not None:
                            shift_store(st, 0)
                        if L["B2"] is not None:
                            store_oT(st, 0)
                    if g == 7 and L["C"] == 0:
                        n = st.n(-1)
                        b, k = st.bank("bcC")
                        after(act, work_free[b], k + 1)
                        affine(st, crm, C_G2, C_B2, n, c_affine, 2 * (n + 1))
                        a.copy(xch[1 - st.par][:, :, :], crm[:, :, :]).then_inc(c_hi, 1)
                    if L["B2"] is not None:
                        exps(st, g)
                        if g == 0:
                            shift_store(st, 1)
                    if g == 5 and st.s0 < SPARE:
                        if L["B2"] is not None:
                            store_oT(st, 0)
                        if L["B1"] is not None:
                            shift_store(st, 0)
                    if g == 1 and L["A"] == 0:
                        query_high(st)
                    if g == q_slot(L, 1):
                        bank, _ = opened(st, "K")
                        after(act, k_written, 32 * st.n(2))
                        a.copy(kp[:, 2, :, :].rearrange("p c t -> p (c t)"), bank[:, :]).then_inc(k_high, 1)
                    if g == 2 and L["R"] is not None:
                        n = st.n(-2)
                        b, k = st.bank("bcR")
                        after(act, work_free[b], k + 1)
                        affine(st, crm, C_SCALE, C_SHIFT, n - B, c_affine, 2 * (n + 1))
                    if g == 3 and L["C"] == 1:
                        bank, free = opened(st, "Wo")
                        if L["R"] is not None:
                            b, k = st.bank("bcR")
                            after(act, work_free[b], k + 1)
                        else:
                            act.wait_ge(z_ready, B)
                        a.copy(flat(y[:, :, :]), bank[:, :]).then_inc(free, 1)
                    if g == 3 and L["V"] is not None:
                        bank, free = opened(st, "V")
                        after(act, pv_done, 4 * st.n(0))
                        a.copy(vaug[1 - st.par][:, :, :, 0:DH],
                               bank[:, :].rearrange("p (t h d) -> p t h d", t=TC, h=H)).then_inc(free, 1)
                    if g == 4 and L["N"] == 1:
                        n = st.n(3)
                        after(act, x1_ready, n - B + 1)
                        a.copy(xnh[1 - st.par][:, :, :],
                               X[:, bass.ds(n - B, 1), :, :].rearrange("p o c t -> p (o c) t")).then_inc(n_hi, 1)
                    if L["C2"] is not None:
                        tanh(st, g)
                        if g >= 1:
                            h_high_part(st, st.n(-2), g - 1)
                    if g == 7 and L["N"] == 0:
                        n = st.n(3)
                        b, k = st.bank("bcN")
                        after(act, work_free[b], k + 1)
                        affine(st, nrm, C_G1, C_B1, n, n_affine, 2 * (n + 1))
                        a.copy(xnh[1 - st.par][:, :, :], nrm[:, :, :]).then_inc(n_hi, 1)
                    m = SWAPS.get((st.s0, g))
                    if m is not None:
                        act.wait_ge(swap_loaded, 16 * (m + 1))
                        b, k = st.bank(("K", "K", "V", "Wo")[m])
                        act.wait_ge(work_full[b], k + 1)
                        a.copy(Wh[:, m, :, :], nrm[:, :, :]).then_inc(swap_hi, 1)
                    if g == 5 and st.s0 in RAW_SPLIT:
                        raw_high(RAW_SPLIT[st.s0])
            def short():
                act.wait_ge(flag_ready, 1)
                return nc.scalar.value_load(short_flag[0:1, 0:1], min_val=0, max_val=1)

            run_steps(nc.scalar, step, short)

        @block.gpsimd
        def _(pool):
            p = nc.gpsimd
            p.memset(ident[:, :], 0.0).then_inc(consts, 1)
            p.memset(ones[:, :], 1.0)
            p.memset(mean1[:, :], 1.0 / D)
            p.memset(three_halves[:, :], 1.5)
            for i in range(2):
                last = p.memset(vaug[i][:, :, :, DH:VW], 0.0)
            last.then_inc(consts, 1)
            pool.wait_ge(consts, 2)
            p.affine_select(out=ident[:, :], in_=ident[:, :], compare_op=ALU.not_equal, fill=1.0, base=0,
                            pattern=[[-1, P]], channel_multiplier=1).then_inc(consts, 1)
            pool.wait_ge(consts, 3)
            p.tensor_copy(identb[:, :], ident[:, :]).then_inc(consts, 1)
            for i in range(2):
                last = p.memset(vaug[i][:, :, :, DH:DH + 1], 1.0)
            last.then_inc(consts, 1)

            def xb(n):
                return X[:, bass.ds(n, 1), :, :].rearrange("p o c t -> p (o c) t")

            def stack_constants(i):
                p.memset(kst[i][PARTS:ROWS, :, :].bitcast(F32), ONE_PAIR).then_inc(stack_ones, 1)
                p.memset(qst[i][PARTS:MASKED, :, :].bitcast(F32), ONE_PAIR).then_inc(stack_ones, 1)
                pool.wait_ge(stack_ones, 3 * i + 1)
                p.memset(kst[i][PARTS:MASKED, :, :].bitcast(F32), 0.0).then_inc(stack_ones, 1)

            def low_q(st, parts, hi_at, lo_at, mid, low):
                n = st.n(2)
                after(pool, mid, n + 1)
                p.tensor_tensor(parts[:, lo_at, :, :], rest[:, :, :], parts[:, 1, :, :],
                                ALU.subtract).then_inc(low, 1)

            def newton_steps(st):
                done = NEWTON_OPS * st.n(3)
                c = slice(0 if st.L["N"] == 0 else 2, 4 if st.L["C"] is not None else 2)
                r, t = rstd[:, c], tmp4[:, c]
                after(pool, guess_ready, st.n(3) + 1)
                for i in range(3):
                    after(pool, newton, done + 4 * i)
                    p.tensor_tensor(t, r, r, ALU.mult).then_inc(newton, 1)
                    after(pool, newton, done + 4 * i + 1)
                    p.tensor_tensor(t, t, half_var[:, c], ALU.mult).then_inc(newton, 1)
                    after(pool, newton, done + 4 * i + 2)
                    p.tensor_tensor(t, t, three_halves[:, c], ALU.add).then_inc(newton, 1)
                    after(pool, newton, done + 4 * i + 3)
                    p.tensor_tensor(r, r, t, ALU.mult).then_inc(newton, 1)

            def step(st):
                L = st.L
                for g in range(SLOTS):
                    if g == 0 and L["C3"] is not None:
                        h_low_part(st.n(-3), HC - 1)
                    if g == 3 and st.s0 == FIRST:
                        pool.wait_ge(sq_n, 1)
                        for i in range(2):
                            stack_constants(i)
                        pool.wait_ge(stack_ones, 6)
                    if g == q_slot(L):
                        low_q(st, qp, 0, 2, q_mid, q_low)
                    if g == 2:
                        if L["N"] == 0:
                            n = st.n(3)
                            after(pool, x_loaded, 16 * (n + 1))
                            after(pool, n_lo, n)
                            p.tensor_tensor(nrm[:, :, :], xb(n), xb(n), ALU.mult).then_inc(sq_n, 1)
                    if g == q_slot(L, 1):
                        low_q(st, kp, 2, 0, k_mid, k_low)
                    if g == 2 and L["R"] is not None:
                        n = st.n(-2)
                        after(pool, c_affine, 2 * (n + 1))
                        p.tensor_tensor(crm[:, :, :], crm[:, :, :], xb(n - B), ALU.add).then_inc(out_ready, 1)
                    if g == 3 and L["C"] is not None:
                        b, k = st.bank("Wo")
                        after(pool, work_free[b], k + 1)
                        b, k = st.bank("bcR") if L["R"] is not None else \
                            st.last().bank("bcN" if st.last().L["N"] == 0 else "bcC")
                        after(pool, work_full[b], k + 1)
                        p.tensor_tensor(dg[:, :, :].rearrange("p (c u) t -> p c (u t)", c=FC),
                                        y[:, :, :], y[:, :, :], ALU.mult).then_inc(sq_c, 1)
                    if g == 4 and L["N"] == 1:
                        n = st.n(3)
                        after(pool, n_hi, n + 1)
                        if L["V"] is not None:
                            b, k = st.bank("V")
                            after(pool, work_full[b], k + 1)
                        p.tensor_tensor(xnl[1 - st.par][:, :, :], xb(n - B),
                                        xnh[1 - st.par][:, :, :].bitcast(F32), ALU.subtract).then_inc(n_lo, 1)
                    if g == 5:
                        if L["N"] == 0 or L["C"] is not None:
                            newton_steps(st)
                        if L["C"] == 0:
                            n = st.n(-1)
                            p.tensor_tensor(xb(n), xb(n), y[:, :, :], ALU.add).then_inc(z_ready, 1)
                    if g == 7 and L["C"] == 0:
                        after(pool, c_hi, st.n(-1) + 1)
                        p.tensor_tensor(xcl[1 - st.par][:, :, :], crm[:, :, :],
                                        xch[1 - st.par][:, :, :].bitcast(F32), ALU.subtract).then_inc(c_lo, 1)
                    if L["C2"] is not None and g >= 1:
                        h_low_part(st.n(-2), g - 1)
                if L["N"] == 0:
                    after(pool, n_hi, st.n(3) + 1)
                    p.tensor_tensor(xnl[1 - st.par][:, :, :], nrm[:, :, :],
                                    xnh[1 - st.par][:, :, :].bitcast(F32), ALU.subtract).then_inc(n_lo, 1)

            def h_low_part(n, i):
                after(pool, h_high, HC * n + i + 1)
                after(pool, down_done, HC * n + i - 1)
                p.tensor_tensor(hl[:, i % 2, :], hf[:, i % 2, :], hh[:, i % 2, :].bitcast(F32),
                                ALU.subtract).then_inc(h_low, 1)

            run_steps(nc.gpsimd, step)


def kernel(**inputs):
    import numpy as np
    import concourse.bacc as bacc
    from concourse.bass_utils import run_bass_kernel_spmd

    a = {k: np.asarray(v) for k, v in inputs.items()}

    def t(name):
        return a[name].T

    def by_dim(name):
        return t(name).reshape(D, FC, H // FC, DH).transpose(0, 1, 3, 2).reshape(D, D)

    def chunks(vec):
        return vec.reshape(-1, P).T

    def words(m):
        return np.ascontiguousarray(m).view(np.int32).reshape(TC, P, T // 4).transpose(1, 0, 2)

    arrays = {
        "xT": a["x"].transpose(2, 0, 1).reshape(FC, P, B * T),
        "w0": np.stack([by_dim("L0_cond_Wq"), by_dim("L0_cond_Wk"), t("L0_cond_Wv"), t("L0_cond_Wo")]),
        "w_ffn": np.stack([t("L0_cond_gate_w"), t("L0_cond_hid_w")]),
        "w_out": t("L0_cond_out_w"),
        "w1": np.stack([by_dim("L1_cond_Wq"), by_dim("L1_cond_Wk"), t("L1_cond_Wv"), t("L1_cond_Wo")]),
        "condT": t("cond_256"),
        "cond_w": np.concatenate([t("L0_cond_g1w"), t("L0_cond_b1w"), t("L0_cond_g2w"), t("L0_cond_b2w"),
                                  t("L1_cond_Wc")], axis=1),
        "cond_b": chunks(np.concatenate([a["L0_cond_g1b"], a["L0_cond_b1b"], a["L0_cond_g2b"],
                                         a["L0_cond_b2b"], a["L1_cond_bc"]])),
        "rms_scale": chunks(a["L1_cond_rms_scale"]),
        "mask": words(a["mask_SxS_bk1"]),
        "maskT": words(a["mask_SxS_bk1"].T),
    }
    arrays = {k: np.ascontiguousarray(v) for k, v in arrays.items()}
    nc = bacc.Bacc("TRN2", target_bir_lowering=False, num_devices=1)
    args = [nc.dram_tensor(k, v.shape, mybir.dt.from_np(v.dtype), kind="ExternalInput").ap()
            for k, v in arrays.items()]
    args.append(nc.dram_tensor("yT", (FC, P, B * T), F32, kind="ExternalOutput").ap())
    build(nc, *args)
    r = run_bass_kernel_spmd(nc, [arrays], core_ids=[0])
    out = np.asarray(r.results[0]["yT"])
    return np.ascontiguousarray(out.reshape(D, B, T).transpose(1, 2, 0))
```
